# Optimizing a Trainium2 kernel written in Bass

```python
import numpy as np
import jax
import jax.numpy as jnp

def _softmax(x, axis=-1):
    return jax.nn.softmax(x, axis=axis)

def _gelu(x):
    return jax.nn.gelu(x, approximate=True)

def _silu(x):
    return jax.nn.silu(x)

def _sigmoid(x):
    return jax.nn.sigmoid(x)

def _layernorm(x, axis=-1, eps=1e-05):
    m = jnp.mean(x, axis=axis, keepdims=True)
    v = jnp.var(x, axis=axis, keepdims=True)
    return (x - m) / jnp.sqrt(v + eps)

def _scatter_add(tgt, idx, src, axis=0):
    return tgt.at[idx].add(src)

def _segment_sum(src, seg, n):
    return jax.ops.segment_sum(src, seg, n)
kernel_name = 'mk_adaln_d1_jaxref_r8_59bf88'

def setup_inputs(seed: int=0):
    np.random.seed(seed)
    _w = jnp.asarray

    def _L0_attn_setup():
        import math
        import jax, jax.numpy as jnp
        import numpy as np
        HEAD_DIM = 128
        NUM_HEADS = 16
        ROPE_BASE = 10000.0

        def _rope_tables(seq_len, dim, dtype):
            inv_freq = 1.0 / ROPE_BASE ** (jnp.arange(0, dim, 2, dtype=jnp.float32) / dim)
            t = jnp.arange(seq_len, dtype=jnp.float32)
            freqs = jnp.einsum('i,j->ij', t, inv_freq)
            emb = jnp.concatenate([freqs, freqs], axis=-1)
            return (jnp.cos(emb).astype(dtype), jnp.sin(emb).astype(dtype))

        def _rotate_half(x):
            x1, x2 = jnp.split(x, 2, axis=-1)
            return jnp.concatenate([-x2, x1], axis=-1)

        def _apply_rope(x, cos, sin):
            return x * cos[None, :, None, :] + _rotate_half(x) * sin[None, :, None, :]
        key = jax.random.key(seed)
        k1, k2, k3 = jax.random.split(key, 3)
        B, S, dim = (2, 256, 256)
        out_dim = (NUM_HEADS + 2 * NUM_HEADS) * HEAD_DIM
        x = jax.random.normal(k1, (B, S, dim), dtype=jnp.float32)
        w_qkv = jax.random.normal(k2, (out_dim, dim), dtype=jnp.float32) * 0.02
        w_out = jax.random.normal(k3, (dim, NUM_HEADS * HEAD_DIM), dtype=jnp.float32) * 0.02
        return {'x': x, 'w_qkv': w_qkv, 'w_out': w_out}
    _L0_attn_in = _L0_attn_setup()

    def _L0_ffn_setup():
        import jax, jax.numpy as jnp
        import numpy as np
        JITTER_EPS = 0.01
        NUM_EXPERTS = 8
        TOP_K = 2
        HIDDEN = 256
        INTER = 512

        def _routing(logits):
            top2_vals, top2_idx = jax.lax.top_k(logits, TOP_K)

            def one_multiplier(thresh, base_scores, sel):
                factor = jnp.maximum(jnp.abs(logits), thresh)
                jitter_mask = (thresh - logits) / factor > 2.0 * JITTER_EPS
                s = jnp.where(jitter_mask, -jnp.inf, base_scores)
                p = jax.nn.softmax(s, axis=-1)
                return jnp.take_along_axis(p, sel[:, None], axis=-1)
            m1 = one_multiplier(top2_vals[:, 0:1], logits, top2_idx[:, 0])
            sel0_onehot = jax.nn.one_hot(top2_idx[:, 0], logits.shape[-1], dtype=bool)
            scores2 = jnp.where(sel0_onehot, -jnp.inf, logits)
            m2 = one_multiplier(top2_vals[:, 1:2], scores2, top2_idx[:, 1])
            multiplier = jnp.concatenate([m1, m2], axis=-1)
            return (multiplier, top2_idx)
        key = jax.random.key(seed)
        ks = jax.random.split(key, 5)
        B, S = (2, 256)
        hidden_states = jax.random.normal(ks[0], (B, S, HIDDEN), dtype=jnp.float32)
        scale_h = 1.0 / np.sqrt(HIDDEN)
        scale_i = 1.0 / np.sqrt(INTER)
        gate_w = jax.random.normal(ks[1], (NUM_EXPERTS, HIDDEN), dtype=jnp.float32) * scale_h
        w1 = jax.random.normal(ks[2], (NUM_EXPERTS, INTER, HIDDEN), dtype=jnp.float32) * scale_h
        w3 = jax.random.normal(ks[3], (NUM_EXPERTS, INTER, HIDDEN), dtype=jnp.float32) * scale_h
        w2 = jax.random.normal(ks[4], (NUM_EXPERTS, HIDDEN, INTER), dtype=jnp.float32) * scale_i
        return {'hidden_states': hidden_states, 'gate_w': gate_w, 'w1': w1, 'w2': w2, 'w3': w3}
    _L0_ffn_in = _L0_ffn_setup()
    _L0_c = _w((lambda *s: np.random.randn(*s).astype(np.float32) * 0.05)(8, 256))
    _L0_wmod = _w((lambda *s: np.random.randn(*s).astype(np.float32) * 0.05)(256, 6 * 256) * 256 ** (-0.5))
    _d = {'L0_attn_x': _L0_attn_in['x'], 'L0_attn_w_qkv': _L0_attn_in['w_qkv'], 'L0_attn_w_out': _L0_attn_in['w_out'], 'L0_ffn_gate_w': _L0_ffn_in['gate_w'], 'L0_ffn_w1': _L0_ffn_in['w1'], 'L0_ffn_w2': _L0_ffn_in['w2'], 'L0_ffn_w3': _L0_ffn_in['w3'], 'L0_c': _L0_c, 'L0_wmod': _L0_wmod}
    _x0 = _d['L0_attn_x']
    _d['L0_attn_x'] = jax.random.normal(jax.random.fold_in(jax.random.key(seed), 1), (8, 256, 256), dtype=_x0.dtype)
    del _x0
    return _d

def reference(L0_attn_x, L0_attn_w_qkv, L0_attn_w_out, L0_ffn_gate_w, L0_ffn_w1, L0_ffn_w2, L0_ffn_w3, L0_c, L0_wmod):

    def _L0_attn_ref(x, w_qkv, w_out):
        import math
        import jax, jax.numpy as jnp
        import numpy as np
        HEAD_DIM = 128
        NUM_HEADS = 16
        ROPE_BASE = 10000.0

        def _rope_tables(seq_len, dim, dtype):
            inv_freq = 1.0 / ROPE_BASE ** (jnp.arange(0, dim, 2, dtype=jnp.float32) / dim)
            t = jnp.arange(seq_len, dtype=jnp.float32)
            freqs = jnp.einsum('i,j->ij', t, inv_freq)
            emb = jnp.concatenate([freqs, freqs], axis=-1)
            return (jnp.cos(emb).astype(dtype), jnp.sin(emb).astype(dtype))

        def _rotate_half(x):
            x1, x2 = jnp.split(x, 2, axis=-1)
            return jnp.concatenate([-x2, x1], axis=-1)

        def _apply_rope(x, cos, sin):
            return x * cos[None, :, None, :] + _rotate_half(x) * sin[None, :, None, :]
        B, S, _ = x.shape
        H, D = (NUM_HEADS, HEAD_DIM)
        qkv = jnp.einsum('bsd,od->bso', x, w_qkv)
        qkv = qkv.reshape(B, S, 3 * H, D)
        q = qkv[:, :, :H, :]
        k = qkv[:, :, H:2 * H, :]
        v = qkv[:, :, 2 * H:, :]
        cos, sin = _rope_tables(S, D, x.dtype)
        q = _apply_rope(q, cos, sin)
        k = _apply_rope(k, cos, sin)
        scale = 1.0 / math.sqrt(D)
        logits = jnp.einsum('bqhd,bkhd->bhqk', q, k) * scale
        attn = jax.nn.softmax(logits.astype(jnp.float32), axis=-1).astype(logits.dtype)
        out = jnp.einsum('bhqk,bkhd->bqhd', attn, v)
        out = out.reshape(B, S, H * D)
        return jnp.einsum('bso,do->bsd', out, w_out)

    def _L0_ffn_ref(hidden_states, gate_w, w1, w2, w3):
        import jax, jax.numpy as jnp
        import numpy as np
        JITTER_EPS = 0.01
        NUM_EXPERTS = 8
        TOP_K = 2
        HIDDEN = 256
        INTER = 512

        def _routing(logits):
            top2_vals, top2_idx = jax.lax.top_k(logits, TOP_K)

            def one_multiplier(thresh, base_scores, sel):
                factor = jnp.maximum(jnp.abs(logits), thresh)
                jitter_mask = (thresh - logits) / factor > 2.0 * JITTER_EPS
                s = jnp.where(jitter_mask, -jnp.inf, base_scores)
                p = jax.nn.softmax(s, axis=-1)
                return jnp.take_along_axis(p, sel[:, None], axis=-1)
            m1 = one_multiplier(top2_vals[:, 0:1], logits, top2_idx[:, 0])
            sel0_onehot = jax.nn.one_hot(top2_idx[:, 0], logits.shape[-1], dtype=bool)
            scores2 = jnp.where(sel0_onehot, -jnp.inf, logits)
            m2 = one_multiplier(top2_vals[:, 1:2], scores2, top2_idx[:, 1])
            multiplier = jnp.concatenate([m1, m2], axis=-1)
            return (multiplier, top2_idx)
        B, S, H = hidden_states.shape
        x = hidden_states.reshape(-1, H)
        logits = jnp.einsum('th,eh->te', x, gate_w)
        multiplier, top2_idx = _routing(logits)
        out = jnp.zeros_like(x)
        for e in range(NUM_EXPERTS):
            w_e = jnp.sum(multiplier * (top2_idx == e), axis=-1)
            h = jax.nn.silu(x @ w1[e].T) * (x @ w3[e].T)
            out = out + w_e[:, None] * (h @ w2[e].T)
        return out.reshape(B, S, H)
    x = L0_attn_x
    mod = (_silu(L0_c) @ L0_wmod).reshape(L0_c.shape[0], 6, 1, -1)
    sa, ca, ga, sb, cb, gb = (mod[:, 0], mod[:, 1], mod[:, 2], mod[:, 3], mod[:, 4], mod[:, 5])
    ga = (2 * (ga >= 0) - 1) * jnp.maximum(jnp.abs(ga), 0.25)
    gb = (2 * (gb >= 0) - 1) * jnp.maximum(jnp.abs(gb), 0.25)
    h = _layernorm(x, axis=-1) * (1 + ca) + sa
    x = x + ga * _L0_attn_ref(h, L0_attn_w_qkv, L0_attn_w_out)
    h = _layernorm(x, axis=-1) * (1 + cb) + sb
    x = x + gb * _L0_ffn_ref(h, L0_ffn_gate_w, L0_ffn_w1, L0_ffn_w2, L0_ffn_w3)
    return x

_drawn_inputs = setup_inputs


def setup_inputs(seed=0):
    import zlib

    import numpy as np

    out = dict(_drawn_inputs(seed))
    spreads = {}
    factors = {'L0_attn_w_qkv': 4.686, 'L0_attn_w_out': 4.424}
    for name, (base, spread) in spreads.items():
        noise = np.random.default_rng([zlib.crc32(name.encode()), seed]).standard_normal(out[name].shape)
        drawn = base * np.exp(spread * noise) if base else spread * noise
        out[name] = jnp.asarray(drawn.astype(out[name].dtype))
    for name, factor in factors.items():
        out[name] = (out[name] * factor).astype(out[name].dtype)
    return out
```

```python
from contextlib import ExitStack

import concourse.bass as bass
from concourse import mybir

F32 = mybir.dt.float32
F16 = mybir.dt.float16
I32 = mybir.dt.int32
ALU = mybir.AluOpType
ACT = mybir.ActivationFunctionType
AX = mybir.AxisListType

P = 128
B, S, D = 8, 256, 256
H, DH = 16, 128
E, F = 8, 512
T = B * S
NT = T // P
TT = S // P
KT = D // P
NMOD = 6
EPS = 1e-5
GATE_FLOOR = 0.25

W_UP = 64.0
V_UP = 16.0
P_UP = 256.0
O_UP = 16.0
PASSES = ((0, 0), (0, 1), (1, 0))

HQ = 4
NG = H // HQ
FT = F // P
FW = 2 * KT * F + FT * D
FPART = FW // NG
NB = 2 * T // P + E - 1
XR = E * T
G_UP = 16.0
FAR = 3.0e38
JITTER = 0.02
M16_AT, EXP_AT, ROUTE_OPS, TABLE_OPS = 13, 14, 26, 24
TABLE = 24 + E * NT + 2 * NB * E
WCOLS = H * 3 * KT * DH
WALL = WCOLS + H * D
NCH = 16
CH = WALL // NCH
STAGES = 4


def build(nc, x, c, wmod, rope, wall, gate_w, fw, table, out, mscr, wscr, xrows, yrows):
    with ExitStack() as ctx:
        def sb(name, shape, dt=F32):
            return ctx.enter_context(nc.sbuf_tensor(name, shape, dt))

        def bank(name):
            return ctx.enter_context(nc.psum_tensor(name, [P, 512], F32))

        def sem(name):
            return ctx.enter_context(nc.semaphore(name))

        arena = sb("arena", [P, E * 2 * FW], F16)
        spans = (2 * WCOLS, 2 * B * KT * S, 2 * H * D, 2 * H * S)
        assert sum(spans) == E * 2 * FW
        cuts = [sum(spans[:i]) for i in range(5)]
        qkv16 = arena[:, cuts[0]:cuts[1]].rearrange("p (a n) -> p a n", a=2)
        hT = arena[:, cuts[1]:cuts[2]].rearrange("p (a b k s) -> p a b k s", a=2, b=B, k=KT)
        wo16 = arena[:, cuts[2]:cuts[3]].rearrange("p (a h n) -> p a h n", a=2, h=H)
        oT = arena[:, cuts[3]:cuts[4]].rearrange("p (a h s) -> p a h s", a=2, h=H)
        wmod_sb = arena[:, cuts[3]:cuts[3] + 2 * KT * NMOD * D].bitcast(F32) \
            .rearrange("p (k n) -> p k n", k=KT)
        xs = sb("xs", [P, NT, D])
        stage = sb("stage", [P, STAGES, CH])
        split16 = sb("split16", [P, 2, FPART], F16)
        rope_sb = sb("rope_sb", [P, 2, TT * 2 * DH])
        c_sb = sb("c_sb", [P, KT * B])
        c_tanh = sb("c_tanh", [P, KT * B])
        c_silu = sb("c_silu", [P, KT, B])
        modT = sb("modT", [P, 2 * KT, B])
        g_sign = sb("g_sign", [B, 2 * D])
        g_abs = sb("g_abs", [B, 2 * D])
        m_row = sb("m_row", [B, 4, D])
        mB = sb("mB", [P, 4, D])
        held = sb("held", [P, 1])
        zeros = sb("zeros", [P, 512])
        stats = sb("stats", [P, NT, 6])
        mv = sb("mv", [P, NT, 2])
        rstd = sb("rstd", [P, NT])
        half_neg = sb("half_neg", [P, NT])
        z = sb("z", [P, TT, D])
        hmod = sb("hmod", [P, KT, S])
        h2 = sb("h2", [P, TT, D])
        h2T = sb("h2T", [P, KT, S])
        gw_sb = sb("gw_sb", [P, KT * E])
        ident = sb("ident", [P, P])
        qkc = sb("qkc", [P, 2, 512])
        rot = sb("rot", [P, 2, 512])
        qkT = sb("qkT", [P, 2, 2, 512], F16)
        v16 = sb("v16", [P, 4, 2, TT * DH], F16)
        ex = sb("ex", [P, 2, TT, S])
        pT = sb("pT", [P, 2, KT, S], F16)
        nmax = sb("nmax", [P, 2, TT])
        esum = sb("esum", [P, 2, TT])
        rsum = sb("rsum", [P, 2, TT])
        gated = sb("gated", [P, TT, D])
        table_sb = sb("table_sb", [P, TABLE])
        tri16 = sb("tri16", [P, P], F16)
        ones16 = sb("ones16", [P, P], F16)
        lg = sb("lg", [P, 2, TT, E])
        hit = sb("hit", [P, TT, E])
        best = sb("best", [P, TT])
        top = sb("top", [P, 2, TT])
        sel = sb("sel", [P, 2, NT, E])
        absl = sb("absl", [P, 2, TT, E])
        diff = sb("diff", [P, 2, TT, E])
        keep = sb("keep", [P, 2, TT, E])
        ediff = sb("ediff", [P, 2, TT, E])
        psum_ = sb("psum_", [P, 2, TT])
        wts = sb("wts", [P, 2, NT])
        m16 = sb("m16", [P, TT, E], F16)
        base = sb("base", [P, E])
        row = sb("row", [P, TT, E])
        srow = sb("srow", [P, 2, TT, E])
        slot = sb("slot", [P, 2, NT])
        slot_i = sb("slot_i", [P, 2, TT], I32)
        cnt = sb("cnt", [P, E])
        over = sb("over", [P, E, NT])
        ends = sb("ends", [P, 2, E])
        shift = sb("shift", [P, E])
        moved = sb("moved", [P, 2 * NT, E])
        ypos = sb("ypos", [P, 2, NT])
        ypos_i = sb("ypos_i", [P, 2, NT], I32)
        bcmp = sb("bcmp", [P, NB, E])
        bexp = sb("bexp", [P, NB])
        brow = sb("brow", [P, NB])
        btab = sb("btab", [P, 2, NB], I32)
        xg = sb("xg", [P, 2, D])
        xT = sb("xT", [P, 2, 2, KT, P], F16)
        th = sb("th", [P, F])
        ua = sb("ua", [P, F])
        gg = sb("gg", [P, F])
        gT = sb("gT", [P, 2, FT, P], F16)
        y_sb = sb("y_sb", [P, 2, D])
        yg = stage[:, 0:2, :].rearrange("p a (j n) -> p (a j) n", n=D) \
            .rearrange("p (r j) n -> p r j n", j=2)
        gbB = stage[:, 2:4, :].rearrange("p a (j n) -> p (a j) n", n=D)

        t_first = table_sb[:, 0:TT * E].rearrange("p (t e) -> p t e", e=E)
        t_base = table_sb[:, 16:24]
        t_thr = table_sb[:, 24:24 + E * NT].rearrange("p (e k) -> p e k", k=NT)
        o = 24 + E * NT
        t_blk = table_sb[:, o:o + NB * E].rearrange("p (k e) -> p k e", e=E)
        t_exp = table_sb[:, o + NB * E:o + 2 * NB * E].rearrange("p (k e) -> p k e", e=E)

        b_qk, b_v, b_t, b_pt, b_s, b_pv, b_acc, b_ln = (
            bank(n) for n in ("b_qk", "b_v", "b_t", "b_pt", "b_s", "b_pv", "b_acc", "b_ln"))

        b_a = (b_qk, b_v)

        x_in, small_in, w_in = sem("x_in"), sem("small_in"), [sem(f"w_in{i}") for i in range(STAGES)]
        w_hi, w_lo = sem("w_hi"), sem("w_lo")
        consts = sem("consts")
        c_t, c_s = sem("c_t"), sem("c_s")
        mod_mm, mod_sb, g_mm, g_done, g_out, m_in = (
            sem(n) for n in ("mod_mm", "mod_sb", "g_mm", "g_done", "g_out", "m_in"))
        ln_stat, ln_mv, ln_rstd, ln_z, ln_t, ln_hi, ln_mod, ln_lo = (
            sem(n) for n in ("ln_stat", "ln_mv", "ln_rstd", "ln_z", "ln_t", "ln_hi", "ln_mod", "ln_lo"))
        qk_mm, v_mm, t_mm, s_mm, pt_mm, pv_mm, o_mm = (
            sem(n) for n in ("qk_mm", "v_mm", "t_mm", "s_mm", "pt_mm", "pv_mm", "o_mm"))
        qk_copied, v_hi, t_hi, exped, pt_hi, o_hi = (
            sem(n) for n in ("qk_copied", "v_hi", "t_hi", "exped", "pt_hi", "o_hi"))
        rot_done, v_lo, t_lo, maxed, rsummed, pt_lo, o_lo, gate_done, x1_done = (
            sem(n) for n in ("rot_done", "v_lo", "t_lo", "maxed", "rsummed", "pt_lo", "o_lo",
                             "gate_done", "x1_done"))
        cos_done, rope_done, normed = sem("cos_done"), sem("rope_done"), sem("normed")
        fw_in, fw_hi, fw_lo, fw_out, w_ffn = (sem(n) for n in ("fw_in", "fw_hi", "fw_lo", "fw_out", "w_ffn"))
        l2_stat, l2_mv, l2_rstd, l2_z, h2_done, h2_t, h2_copy, logit_mm, rt, rt_exp, rank_mm = (
            sem(n) for n in ("l2_stat", "l2_mv", "l2_rstd", "l2_z", "h2_done", "h2_t", "h2_copy",
                             "logit_mm", "rt", "rt_exp", "rank_mm"))
        zeroed, scattered, bt, btab_done = sem("zeroed"), sem("scattered"), sem("bt"), sem("btab_done")
        xg_in = [sem(f"xg_in{i}") for i in range(2)]
        y_st = [sem(f"y_st{i}") for i in range(2)]
        xt_mm, a_mm, gt_mm, b_mm, y_mm = (sem(n) for n in ("xt_mm", "a_mm", "gt_mm", "b_mm", "y_mm"))
        x_hi, tanhed, g_hi, y_out = (sem(n) for n in ("x_hi", "tanhed", "g_hi", "y_out"))
        x_lo, u_done, g_lo, gg_done = (sem(n) for n in ("x_lo", "u_done", "g_lo", "gg_done"))
        yg_in = [sem(f"yg_in{i}") for i in range(4)]
        gb_in, fin, fin_done, stored = sem("gb_in"), sem("fin"), sem("fin_done"), sem("stored")

        block = ctx.enter_context(nc.Block())

        def all_steps(step, late, eng):
            for i in range(-4, HQ):
                step(i, i % 4, 0, i, 0)
            with eng.Fori(1, NG - 1) as g:
                trip(step, 0, g)
            with eng.Fori(0, B - 1) as b:
                trip(step, b, NG - 1)
                late(b, 0)
                with eng.Fori(0, NG - 2) as g:
                    trip(step, b + 1, g)
                late(b, 1)
                trip(step, b + 1, NG - 2, {0: lambda: late(b, 2), 1: lambda: late(b, 3)})
                late(b, 4)
            trip(step, B - 1, NG - 1)
            for part in range(5):
                late(B - 1, part)

        def trip(step, b, g, between={}):
            for j in range(HQ):
                step(b * H + (g * HQ + j), j, b, g * HQ + j, g)
                if j in between:
                    between[j]()

        def head_out(half, h):
            if isinstance(h, int):
                return oT[:, half, h, :]
            return oT[:, half, bass.ds(h, 1), :].squeeze(1)

        def exists(i, ahead):
            return not isinstance(i, int) or 0 <= i + ahead < B * H

        def at(i, b, h, ahead):
            if isinstance(i, int):
                return divmod(i + ahead, H)
            if not isinstance(h, int) or h + ahead < H:
                return b, h + ahead
            return b + 1, h + ahead - H

        def wait(eng, s, value):
            if not (isinstance(value, int) and value <= 0):
                eng.wait_ge(s, value)

        def all_blocks(step, eng):
            for k in range(-2, 2):
                step(k, k % 2, (k - k % 2) // 2)
            with eng.Fori(1, (NB - 5) // 2) as r:
                for j in range(2):
                    step(r * 2 + j, j, r)
            for k in range((NB - 5) // 2 * 2, NB):
                step(k, k % 2, k // 2)

        def has(k, ahead):
            return not isinstance(k, int) or 0 <= k + ahead < NB

        @block.sync
        def _(sp):
            sp.dma_start(xs[:, :, :], x.rearrange("(t p) n -> p t n", p=P)).then_inc(x_in, 16)
            for k in range(STAGES):
                sp.dma_start(stage[:, k, :], wall[:, k * CH:(k + 1) * CH]).then_inc(w_in[k], 16)
            with sp.Fori(1, NCH // STAGES) as r:
                for k in range(STAGES):
                    sp.wait_ge(w_lo, r * STAGES + (k + 1 - STAGES))
                    sp.dma_start(stage[:, k, :], wall[:, bass.ds((r * STAGES + k) * CH, CH)]) \
                        .then_inc(w_in[k], 16)
            sp.wait_ge(w_lo, NCH - STAGES + 1)
            sp.dma_start(stage[:, 0, 0:FPART], fw[0, :, 0:FPART]).then_inc(fw_in, 16)
            sp.wait_ge(g_out, 16)
            sp.dma_start(mB[:, :, :], mscr[0:1, :].partition_broadcast(P)).then_inc(m_in, 16)

            def part_out(b, g):
                sp.wait_ge(fw_lo, b * NG + (g + 1))
                dst = wscr[b, :, :, g * FPART:(g + 1) * FPART] if isinstance(b, int) else \
                    wscr[bass.ds(b, 1), :, :, g * FPART:(g + 1) * FPART].squeeze(0)
                sp.dma_start(dst, split16[:, :, :]).then_inc(fw_out, 16)

            def part_in(b, g):
                src = fw[b, :, g * FPART:(g + 1) * FPART] if isinstance(b, int) else \
                    fw[bass.ds(b, 1), :, g * FPART:(g + 1) * FPART].squeeze(0)
                sp.dma_start(stage[:, 0, 0:FPART], src).then_inc(fw_in, 16)

            def next_part(b, g):
                part_out(b, g)
                if isinstance(g, int) and g + 1 < NG:
                    part_in(b, g + 1)
                elif not isinstance(b, int):
                    part_in(b + 1, 0)

            next_part(0, 0)
            next_part(0, 1)
            with sp.Fori(1, B) as b:
                next_part(b - 1, 2)
                next_part(b - 1, 3)
                next_part(b, 0)
                next_part(b, 1)
                sp.wait_ge(h2_done, b * 2)
                sp.dma_start(mB[:, :, :], mscr[bass.ds(b, 1), :].partition_broadcast(P)).then_inc(m_in, 16)
            next_part(B - 1, 2)
            next_part(B - 1, 3)
            sp.wait_ge(fw_out, 16 * B * NG)
            sp.wait_ge(v_mm, B * H)
            sp.wait_ge(qk_mm, B * H)
            for e in range(E):
                if e * 2 * FW + 2 * FW > cuts[2]:
                    sp.wait_ge(o_mm, B)
                sp.dma_start(arena[:, e * 2 * FW:(e + 1) * 2 * FW],
                             wscr[e].rearrange("p a n -> p (a n)")).then_inc(w_ffn, 16)
                sp.wait_ge(w_ffn, 16 * (e + 1))
            sp.dma_start(gbB, mscr[:, D:2 * D].unsqueeze(0).partition_broadcast(P)).then_inc(gb_in, 16)
            for b in range(B):
                sp.wait_ge(fin_done, (b + 1) * TT)
                sp.dma_start(out[b].rearrange("(t p) n -> p t n", p=P), xs[:, b * TT:(b + 1) * TT, :]) \
                    .then_inc(stored, 16)
            sp.wait_ge(stored, 16 * B)

        @block.gpsimd
        def _(pool):
            pool.memset(ident[:, :], 0.0).then_inc(consts, 1)
            pool.memset(tri16[:, :], 1.0).then_inc(consts, 1)
            pool.memset(half_neg[:, :], -0.5).then_inc(consts, 1)
            pool.memset(zeros[:, :], 0.0).then_inc(consts, 1)
            pool.memset(ones16[:, :], 1.0).then_inc(consts, 1)
            pool.wait_ge(consts, 5)
            pool.affine_select(out=ident[:, :], in_=ident[:, :], compare_op=ALU.not_equal, fill=1.0,
                               base=0, pattern=[[-1, P]], channel_multiplier=1).then_inc(consts, 1)
            pool.affine_select(out=tri16[:, :], in_=tri16[:, :], compare_op=ALU.is_gt, fill=0.0,
                               base=0, pattern=[[1, P]], channel_multiplier=-1).then_inc(consts, 1)
            pool.wait_ge(ln_mv, NT + 1)
            pool.tensor_tensor(rstd[:, :], mv[:, :, 1], half_neg[:, :], ALU.pow).then_inc(ln_rstd, 1)
            pool.wait_ge(w_lo, NCH)
            rows = XR // P * D
            xflat = xrows.rearrange("(p r) n -> p (r n)", p=P)
            for q in range(4):
                n = rows // 4
                pool.dma_start(xflat[:, q * n:(q + 1) * n].rearrange("p (r n) -> p r n", n=512),
                               zeros[:, :].unsqueeze(1).to_broadcast([P, n // 512, 512])).then_inc(zeroed, 16)

            def step(i, j, b, h, g):
                if exists(i, 4):
                    k = j % 2
                    pool.wait_ge(qk_copied, i + 5)
                    pool.tensor_tensor(qkc[:, k, :], qkc[:, k, :], rope_sb[:, 0, :], ALU.mult) \
                        .then_inc(cos_done, 1)
                    pool.wait_ge(cos_done, i + 5)
                    pool.wait_ge(rot_done, i + 5)
                    pool.tensor_tensor(rot[:, k, :], qkc[:, k, :], rot[:, k, :], ALU.add) \
                        .then_inc(rope_done, 1)
                if exists(i, 2):
                    e = ex[:, (j + 2) % 2, :, :]
                    pool.wait_ge(rsummed, i + 3)
                    pool.tensor_tensor(e, e, rsum[:, (j + 2) % 2, :].unsqueeze(2).to_broadcast([P, TT, S]),
                                       ALU.mult).then_inc(normed, 1)

            def late(b, part):
                if part == 0:
                    pool.wait_ge(l2_mv, (b + 1) * (TT + 1))
                    pool.tensor_tensor(rstd[:, 0:TT], mv[:, 0:TT, 1], half_neg[:, 0:TT], ALU.pow) \
                        .then_inc(l2_rstd, 1)
                if part == 1:
                    pool.wait_ge(l2_z, (b + 1) * TT)
                    pool.wait_ge(m_in, (b + 1) * 16)
                    pool.tensor_tensor(h2[:, :, :], z[:, :, :], mB[:, 2:3, :].to_broadcast([P, TT, D]),
                                       ALU.mult).then_inc(h2_done, 1)
                    pool.wait_ge(h2_done, b * 2 + 1)
                    pool.tensor_tensor(h2[:, :, :], h2[:, :, :], mB[:, 3:4, :].to_broadcast([P, TT, D]),
                                       ALU.add).then_inc(h2_done, 1)
                if part == 4:
                    pool.wait_ge(h2_done, b * 2 + 2)
                    pool.wait_ge(rt, (b + 1) * ROUTE_OPS)
                    pool.wait_ge(zeroed, 64)
                    pool.tensor_tensor(held[:, :], half_neg[:, 0:1], half_neg[:, 1:2], ALU.mult)
                    for q in range(2):
                        for t in range(TT):
                            pool.indirect_dma_start(
                                xrows, bass.IndirectOffsetOnAxis(ap=slot_i[:, q, t:t + 1], axis=0),
                                h2[:, t, :], None).then_inc(scattered, 16)
                    pool.wait_ge(scattered, (b + 1) * 2 * TT * 16)

            all_steps(step, late, pool)

            def put(k, j, r):
                if has(k, 0):
                    pool.wait_ge(y_out, k + 1)
                    pool.dma_start(yrows[bass.ds(k * P, P), :], y_sb[:, j, :]).then_inc(y_st[j], 16)

            all_blocks(put, pool)
            for j in range(2):
                pool.wait_ge(y_st[j], 16 * ((NB + 1 - j) // 2))
            pool.wait_ge(bt, TABLE_OPS)

            def gather(t, k):
                for q in range(2):
                    pool.indirect_dma_start(
                        yg[:, k, q, :], None, yrows,
                        bass.IndirectOffsetOnAxis(ap=ypos_i[:, q, t:t + 1], axis=0)) \
                        .then_inc(yg_in[k], 16)

            for k in range(4):
                gather(k, k)
            for t in range(4, NT):
                pool.wait_ge(fin_done, t - 3)
                gather(t, t % 4)

        @block.scalar
        def _(act):
            act.dma_start(c_sb[:, :], c).then_inc(small_in, 16)
            act.dma_start(wmod_sb, wmod).then_inc(small_in, 16)
            act.dma_start(rope_sb[:, :, :], rope).then_inc(small_in, 16)
            act.dma_start(gw_sb[:, :], gate_w).then_inc(small_in, 16)
            act.dma_start(table_sb[:, :], table).then_inc(small_in, 16)
            act.wait_ge(small_in, 80)
            act.activation(c_tanh[:, :], c_sb[:, :], ACT.Tanh, scale=0.5).then_inc(c_t, 1)
            act.wait_ge(g_done, 3)
            act.dma_start(mscr, m_row[:, :, :].rearrange("b k n -> b (k n)")).then_inc(g_out, 16)
            act.wait_ge(mod_sb, 5)
            with act.Fori(0, B) as b:
                act.wait_ge(ln_t, b + 1)
                for kt in range(KT):
                    act.activation(hT[:, 0, bass.ds(b, 1), kt, :].squeeze(1), b_ln[:, kt * S:(kt + 1) * S],
                                   ACT.Identity, bias=modT[:, kt, bass.ds(b, 1)],
                                   scale=modT[:, KT + kt, bass.ds(b, 1)]).then_inc(ln_hi, 1)
            with act.Fori(0, (NCH * CH - H * D) // CH // STAGES) as r:
                for k in range(STAGES):
                    act.wait_ge(w_in[k], r * 16 + 16)
                    act.activation(qkv16[:, 0, bass.ds((r * STAGES + k) * CH, CH)], stage[:, k, :],
                                   ACT.Copy, scale=W_UP).then_inc(w_hi, 1)
            for k in range(STAGES):
                act.wait_ge(w_in[k], NCH // STAGES * 16)
                act.activation(wo16[:, 0, k * HQ:(k + 1) * HQ, :], stage[:, k, :].rearrange("p (h n) -> p h n", n=D),
                               ACT.Copy, scale=W_UP).then_inc(w_hi, 1)

            def step(i, j, b, h, g):
                if exists(i, 2):
                    act.wait_ge(t_mm, i + 3)
                    wait(act, s_mm, i + 1)
                    act.activation(qkT[:, j % 2, 0, :], b_t[:, :], ACT.Copy).then_inc(t_hi, 1)
                if exists(i, 3):
                    act.wait_ge(v_mm, i + 4)
                    wait(act, pv_mm, i)
                    act.activation(v16[:, (j + 3) % 4, 0, :], b_v[:, 0:TT * DH], ACT.Copy,
                                   scale=V_UP / W_UP).then_inc(v_hi, 1)
                if exists(i, 4):
                    act.wait_ge(qk_mm, i + 5)
                    wait(act, rope_done, i + 3)
                    act.activation(qkc[:, j % 2, :], b_qk[:, :], ACT.Copy).then_inc(qk_copied, 1)
                if exists(i, 0):
                    act.wait_ge(pv_mm, i + 1)
                    act.activation(head_out(0, h), b_pv[:, 0:S], ACT.Copy,
                                   scale=O_UP / (P_UP * V_UP)).then_inc(o_hi, 1)
                if exists(i, 1):
                    act.wait_ge(pt_mm, i + 2)
                    wait(act, pv_mm, i + 1)
                    act.activation(pT[:, 0, :, :], b_pt[:, :].rearrange("p (k s) -> p k s", k=KT),
                                   ACT.Copy, scale=P_UP).then_inc(pt_hi, 1)
                if exists(i, 2):
                    k = j % 2
                    act.wait_ge(maxed, i + 3)
                    wait(act, pt_mm, i + 1)
                    wait(act, rsummed, i + 1)
                    for t in range(TT):
                        e = act.activation(ex[:, k, t, :], b_s[:, t * S:(t + 1) * S], ACT.Exp,
                                           bias=nmax[:, k, t:t + 1], accum_out=esum[:, k, t:t + 1])
                    e.then_inc(exped, 1)
                if j == HQ - 1 and exists(i, 0):
                    part = b * NG + g
                    act.wait_ge(fw_in, part * 16 + 16)
                    wait(act, fw_out, part * 16)
                    act.activation(split16[:, 0, :], stage[:, 0, 0:FPART], ACT.Copy, scale=W_UP) \
                        .then_inc(fw_hi, 1)

            def late(b, part):
                if part == 2:
                    act.wait_ge(h2_t, b + 1)
                    act.activation(h2T[:, :, :], b_ln[:, :].rearrange("p (k s) -> p k s", k=KT), ACT.Copy) \
                        .then_inc(h2_copy, 1)
                if part == 4:
                    act.wait_ge(rt, b * ROUTE_OPS + EXP_AT)
                    act.activation(ediff[:, :, :, :], diff[:, :, :, :], ACT.Exp).then_inc(rt_exp, 1)

            all_steps(step, late, act)
            act.wait_ge(btab_done, 1)
            act.wait_ge(scattered, B * 2 * TT * 16)

            def get(k, slot):
                start = act.value_load(btab[0:1, 1, bass.ds(k, 1)], min_val=0, max_val=XR - P)
                act.dma_start(xg[:, slot, :], xrows[bass.ds(start, P), :]).then_inc(xg_in[slot], 16)

            get(0, 0)
            get(1, 1)

            def ffn(k, j, r):
                if has(k, 2):
                    act.wait_ge(xt_mm, k + 3)
                    wait(act, b_mm, k + 1)
                    act.activation(xT[:, j, 0, :, :], b_t[:, 0:D].rearrange("p (k s) -> p k s", k=KT),
                                   ACT.Copy).then_inc(x_hi, 1)
                if has(k, 4):
                    get(k + 4, j)
                if has(k, 0):
                    act.wait_ge(gt_mm, k + 1)
                    wait(act, y_mm, k)
                    act.activation(gT[:, 0, :, :], b_pt[:, :].rearrange("p (k s) -> p k s", k=FT), ACT.Copy,
                                   scale=G_UP / (2 * W_UP * W_UP)).then_inc(g_hi, 1)
                if has(k, 1):
                    act.wait_ge(a_mm, k + 2)
                    wait(act, u_done, k + 1)
                    act.activation(th[:, :], b_a[(j + 1) % 2][:, :], ACT.Tanh, scale=0.5 / W_UP) \
                        .then_inc(tanhed, 1)
                if has(k, 0):
                    act.wait_ge(y_mm, k + 1)
                    wait(act, y_st[j], r * 16)
                    act.activation(y_sb[:, j, :], b_pv[:, 0:D], ACT.Copy).then_inc(y_out, 1)

            all_blocks(ffn, act)

        @block.vector
        def _(dve):
            dve.wait_ge(x_in, 16)
            for t in range(NT):
                dve.bn_stats(stats[:, t, :], xs[:, t, :]).then_inc(ln_stat, 1)
            dve.wait_ge(ln_stat, NT)
            for t in range(NT):
                dve.bn_aggr(mv[:, t, :], stats[:, t, :]).then_inc(ln_mv, 1)
            dve.wait_ge(ln_mv, NT)
            dve.tensor_scalar(mv[:, :, 1], mv[:, :, 1], EPS, None, ALU.add).then_inc(ln_mv, 1)
            dve.wait_ge(c_t, 1)
            dve.wait_ge(small_in, 80)
            dve.scalar_tensor_tensor(out=c_tanh[:, :], in0=c_tanh[:, :], scalar=1.0, in1=c_sb[:, :],
                                     op0=ALU.add, op1=ALU.mult).then_inc(c_s, 1)
            dve.tensor_copy(base[:, :], t_base)
            dve.wait_ge(c_s, 1)
            dve.tensor_scalar(c_silu[:, :, :], c_tanh[:, :].rearrange("p (k b) -> p k b", k=KT), 0.5, None,
                              ALU.mult).then_inc(c_s, 1)
            dve.wait_ge(g_mm, 1)
            assert O_UP == G_UP
            unit = 1.0 / (W_UP * O_UP)
            dve.tensor_scalar(g_sign[:, :], b_acc[0:B, :], 0.0, 2.0 * unit, ALU.is_ge, ALU.mult) \
                .then_inc(mod_sb, 1)
            dve.tensor_scalar(g_abs[:, :], b_acc[0:B, :], -1.0, GATE_FLOOR, ALU.mult, ALU.max) \
                .then_inc(mod_sb, 1)
            dve.wait_ge(mod_sb, 2)
            dve.tensor_tensor(g_abs[:, :], b_acc[0:B, :], g_abs[:, :], ALU.max).then_inc(mod_sb, 1)
            dve.wait_ge(mod_sb, 3)
            dve.scalar_tensor_tensor(out=m_row[:, 0:2, :], in0=g_sign[:, :].rearrange("b (k n) -> b k n", k=2),
                                     scalar=-unit, in1=g_abs[:, :].rearrange("b (k n) -> b k n", k=2),
                                     op0=ALU.add, op1=ALU.mult).then_inc(g_done, 1)
            dve.tensor_scalar(m_row[:, 2, :], b_v[0:B, 0:D], 1.0, None, ALU.add).then_inc(g_done, 1)
            dve.tensor_copy(m_row[:, 3, :], b_v[0:B, D:2 * D]).then_inc(g_done, 1)
            dve.wait_ge(mod_mm, 1)
            mod_ps = b_qk[:, 0:2 * KT * B].rearrange("p (m b) -> p m b", b=B)
            dve.tensor_copy(modT[:, 0:KT, :], mod_ps[:, 0:KT, :]).then_inc(mod_sb, 1)
            dve.tensor_scalar(modT[:, KT:2 * KT, :], mod_ps[:, KT:2 * KT, :], 1.0, None, ALU.add) \
                .then_inc(mod_sb, 1)
            dve.wait_ge(mod_sb, 5)
            dve.wait_ge(ln_rstd, 1)

            def normalise(b, done):
                for t in range(TT):
                    tile = bass.ds(b * TT + t, 1)
                    dve.tensor_scalar(z[:, t, :], xs[:, tile, :].squeeze(1),
                                      mv[:, tile, 0:1].squeeze(1), rstd[:, tile],
                                      ALU.subtract, ALU.mult).then_inc(done, 1)

            with dve.Fori(0, B) as b:
                normalise(b, ln_z)
                dve.wait_ge(ln_hi, b * KT + KT)
                for kt in range(KT):
                    dve.tensor_scalar(hmod[:, kt, :], b_ln[:, kt * S:(kt + 1) * S],
                                      modT[:, KT + kt, bass.ds(b, 1)], modT[:, kt, bass.ds(b, 1)],
                                      ALU.mult, ALU.add).then_inc(ln_mod, 1)
                dve.wait_ge(ln_mod, b * KT + KT)
                dve.tensor_tensor(hT[:, 1, bass.ds(b, 1), :, :].squeeze(1), hmod[:, :, :],
                                  hT[:, 0, bass.ds(b, 1), :, :].squeeze(1), ALU.subtract).then_inc(ln_lo, 1)
            with dve.Fori(0, (NCH * CH - H * D) // CH // STAGES) as r:
                for k in range(STAGES):
                    dve.wait_ge(w_hi, r * STAGES + (k + 1))
                    part = bass.ds((r * STAGES + k) * CH, CH)
                    dve.scalar_tensor_tensor(out=qkv16[:, 1, part], in0=stage[:, k, :], scalar=W_UP,
                                             in1=qkv16[:, 0, part], op0=ALU.mult, op1=ALU.subtract) \
                        .then_inc(w_lo, 1)
            for k in range(STAGES):
                dve.wait_ge(w_hi, NCH - STAGES + k + 1)
                dve.scalar_tensor_tensor(out=wo16[:, 1, k * HQ:(k + 1) * HQ, :],
                                         in0=stage[:, k, :].rearrange("p (h n) -> p h n", n=D), scalar=W_UP,
                                         in1=wo16[:, 0, k * HQ:(k + 1) * HQ, :], op0=ALU.mult,
                                         op1=ALU.subtract).then_inc(w_lo, 1)

            def low_half(out, full, scale, hi):
                return dve.scalar_tensor_tensor(out=out, in0=full, scalar=scale, in1=hi,
                                                op0=ALU.mult, op1=ALU.subtract)

            qk4 = b_qk[:, :].rearrange("p (a f d) -> p a f d", a=TT * 2, f=2)

            def step(i, j, b, h, g):
                if exists(i, 2):
                    dve.wait_ge(t_hi, i + 3)
                    low_half(qkT[:, j % 2, 1, :], b_t[:, :], 1.0, qkT[:, j % 2, 0, :]).then_inc(t_lo, 1)
                if exists(i, 3):
                    k = (j + 3) % 4
                    dve.wait_ge(v_hi, i + 4)
                    low_half(v16[:, k, 1, :], b_v[:, 0:TT * DH], V_UP / W_UP, v16[:, k, 0, :]) \
                        .then_inc(v_lo, 1)
                if exists(i, 4):
                    k = j % 2
                    dve.wait_ge(qk_copied, i + 5)
                    wait(dve, t_mm, i + 3)
                    r4 = rot[:, k, :].rearrange("p (a f d) -> p a f d", a=TT * 2, f=2)
                    s4 = rope_sb[:, 1, :].rearrange("p (a f d) -> p a f d", a=TT * 2, f=2)
                    dve.tensor_tensor(r4[:, :, 0, :], qk4[:, :, 1, :], s4[:, :, 0, :], ALU.mult)
                    dve.tensor_tensor(r4[:, :, 1, :], qk4[:, :, 0, :], s4[:, :, 1, :], ALU.mult) \
                        .then_inc(rot_done, 1)
                if exists(i, 0):
                    dve.wait_ge(o_hi, i + 1)
                    low_half(head_out(1, h), b_pv[:, 0:S], O_UP / (P_UP * V_UP), head_out(0, h)) \
                        .then_inc(o_lo, 1)
                if exists(i, 2):
                    dve.wait_ge(s_mm, i + 3)
                    wait(dve, exped, i + 1)
                    dve.tensor_reduce(nmax[:, j % 2, :], b_s[:, :].rearrange("p (t s) -> p t s", t=TT),
                                      AX.X, ALU.max, negate=True).then_inc(maxed, 1)
                if exists(i, 1):
                    dve.wait_ge(pt_hi, i + 2)
                    low_half(pT[:, 1, :, :], b_pt[:, :].rearrange("p (k s) -> p k s", k=KT), P_UP,
                             pT[:, 0, :, :]).then_inc(pt_lo, 1)
                if exists(i, 2):
                    dve.wait_ge(exped, i + 3)
                    wait(dve, normed, i + 1)
                    dve.reciprocal(rsum[:, j % 2, :], esum[:, j % 2, :]).then_inc(rsummed, 1)
                if j == HQ - 1 and exists(i, 0):
                    dve.wait_ge(fw_hi, b * NG + g + 1)
                    low_half(split16[:, 1, :], stage[:, 0, 0:FPART], W_UP, split16[:, 0, :]) \
                        .then_inc(fw_lo, 1)

            def late(b, part):
                tiles = bass.ds(b * TT, TT)
                done = [0]

                def link(ins):
                    done[0] += 1
                    ins.then_inc(rt, 1)
                    dve.wait_ge(rt, b * ROUTE_OPS + done[0])

                if part == 0:
                    dve.wait_ge(o_mm, b + 1)
                    dve.wait_ge(m_in, (b + 1) * 16)
                    dve.tensor_tensor(gated[:, :, :], b_acc[:, :].rearrange("p (t n) -> p t n", t=TT),
                                      mB[:, 0:1, :].to_broadcast([P, TT, D]), ALU.mult) \
                        .then_inc(gate_done, 1)
                    dve.wait_ge(gate_done, b + 1)
                    dve.tensor_tensor(z[:, :, :], xs[:, tiles, :], gated[:, :, :], ALU.add) \
                        .then_inc(x1_done, 1)
                    dve.wait_ge(x1_done, b + 1)
                    for t in range(TT):
                        dve.bn_stats(stats[:, t, :], z[:, t, :]).then_inc(l2_stat, 1)
                    dve.wait_ge(l2_stat, (b + 1) * TT)
                    dve.tensor_tensor(xs[:, tiles, :], xs[:, tiles, :], gated[:, :, :], ALU.add)
                    for t in range(TT):
                        dve.bn_aggr(mv[:, t, :], stats[:, t, :]).then_inc(l2_mv, 1)
                    dve.wait_ge(l2_mv, b * (TT + 1) + TT)
                    dve.tensor_scalar(mv[:, 0:TT, 1], mv[:, 0:TT, 1], EPS, None, ALU.add).then_inc(l2_mv, 1)
                if part == 1:
                    dve.wait_ge(l2_rstd, b + 1)
                    for t in range(TT):
                        dve.tensor_scalar(z[:, t, :], z[:, t, :], mv[:, t, 0:1], rstd[:, t:t + 1],
                                          ALU.subtract, ALU.mult).then_inc(l2_z, 1)
                if part == 3:
                    dve.wait_ge(logit_mm, b + 1)
                    link(dve.tensor_copy(lg[:, 0, :, :], b_ln[:, 0:TT * E].rearrange("p (t e) -> p t e", e=E)))
                    for q in range(2):
                        link(dve.tensor_reduce(top[:, q, :], lg[:, q, :, :], AX.X, ALU.max))
                        link(dve.tensor_tensor(hit[:, :, :], lg[:, q, :, :],
                                               top[:, q, :].unsqueeze(2).to_broadcast([P, TT, E]), ALU.is_equal))
                        link(dve.tensor_tensor(hit[:, :, :], hit[:, :, :], t_first, ALU.mult))
                        link(dve.tensor_reduce(best[:, :], hit[:, :, :], AX.X, ALU.max))
                        link(dve.tensor_tensor(sel[:, q, tiles, :], hit[:, :, :],
                                               best[:, :].unsqueeze(2).to_broadcast([P, TT, E]), ALU.is_equal))
                        if q == 0:
                            link(dve.scalar_tensor_tensor(out=lg[:, 1, :, :], in0=sel[:, 0, tiles, :], scalar=-FAR,
                                                          in1=lg[:, 0, :, :], op0=ALU.mult, op1=ALU.add))
                    link(dve.tensor_tensor(m16[:, :, :], sel[:, 0, tiles, :], sel[:, 1, tiles, :], ALU.add))
                    assert done[0] == M16_AT
                    topb = top[:, :, :].unsqueeze(3).to_broadcast([P, 2, TT, E])
                    link(dve.tensor_tensor(diff[:, :, :, :], lg[:, :, :, :], topb, ALU.subtract))
                    assert done[0] == EXP_AT
                if part == 4:
                    done[0] = EXP_AT
                    link(dve.scalar_tensor_tensor(out=absl[:, :, :, :], in0=lg[:, :, :, :], scalar=-1.0,
                                                  in1=lg[:, :, :, :], op0=ALU.mult, op1=ALU.max))
                    topb = top[:, :, :].unsqueeze(3).to_broadcast([P, 2, TT, E])
                    link(dve.tensor_tensor(absl[:, :, :, :], absl[:, :, :, :], topb, ALU.max))
                    link(dve.scalar_tensor_tensor(out=keep[:, :, :, :], in0=absl[:, :, :, :], scalar=-JITTER,
                                                  in1=diff[:, :, :, :], op0=ALU.mult, op1=ALU.is_le))
                    dve.wait_ge(rt_exp, b + 1)
                    link(dve.tensor_tensor(keep[:, :, :, :], keep[:, :, :, :], ediff[:, :, :, :], ALU.mult))
                    link(dve.tensor_reduce(psum_[:, :, :], keep[:, :, :, :], AX.X, ALU.add))
                    link(dve.reciprocal(wts[:, :, tiles], psum_[:, :, :]))
                    dve.wait_ge(rank_mm, b + 1)
                    ranks = b_ln[:, 32:32 + (TT + 1) * E].rearrange("p (t e) -> p t e", e=E)
                    link(dve.tensor_tensor(row[:, :, :], ranks[:, 0:TT, :],
                                           base[:, :].unsqueeze(1).to_broadcast([P, TT, E]), ALU.add))
                    link(dve.tensor_tensor(base[:, :], base[:, :], ranks[:, TT, :], ALU.add))
                    for q in range(2):
                        link(dve.tensor_tensor(srow[:, q, :, :], sel[:, q, tiles, :], row[:, :, :], ALU.mult))
                    link(dve.tensor_reduce(slot[:, :, tiles], srow[:, :, :, :], AX.X, ALU.add))
                    link(dve.tensor_scalar(slot_i[:, :, :], slot[:, :, tiles], 1.0, None, ALU.mult))
                    assert done[0] == ROUTE_OPS

            all_steps(step, late, dve)

            steps = [0]

            def link(ins):
                steps[0] += 1
                ins.then_inc(bt, 1)
                dve.wait_ge(bt, steps[0])

            def over_blocks(v):
                return v.unsqueeze(1).to_broadcast([P, NB, E])

            link(dve.tensor_tensor(cnt[:, :], base[:, :], t_base, ALU.subtract))
            link(dve.tensor_tensor(over[:, :, :], cnt[:, :].unsqueeze(2).to_broadcast([P, E, NT]), t_thr,
                                   ALU.is_gt))
            link(dve.tensor_reduce(cnt[:, :], over[:, :, :], AX.X, ALU.add))
            link(dve.tensor_copy(ends[:, 0, :], cnt[:, :]))
            q = 0
            for d in (1, 2, 4):
                link(dve.tensor_copy(ends[:, 1 - q, 0:d], ends[:, q, 0:d]))
                link(dve.tensor_tensor(ends[:, 1 - q, d:E], ends[:, q, d:E], ends[:, q, 0:E - d], ALU.add))
                q = 1 - q
            link(dve.tensor_tensor(shift[:, :], ends[:, q, :], cnt[:, :], ALU.subtract))
            link(dve.scalar_tensor_tensor(out=shift[:, :], in0=shift[:, :], scalar=float(P), in1=t_base,
                                          op0=ALU.mult, op1=ALU.subtract))
            link(dve.tensor_tensor(bcmp[:, :, :], t_blk, over_blocks(ends[:, q, :]), ALU.is_ge))
            link(dve.tensor_reduce(bexp[:, :], bcmp[:, :, :], AX.X, ALU.add))
            link(dve.tensor_scalar(bexp[:, :], bexp[:, :], E - 1.0, None, ALU.min))
            link(dve.tensor_tensor(bcmp[:, :, :], t_exp, bexp[:, :].unsqueeze(2).to_broadcast([P, NB, E]),
                                   ALU.is_equal))
            link(dve.tensor_tensor(bcmp[:, :, :], bcmp[:, :, :], over_blocks(shift[:, :]), ALU.mult))
            link(dve.tensor_reduce(brow[:, :], bcmp[:, :, :], AX.X, ALU.add))
            link(dve.scalar_tensor_tensor(out=brow[:, :], in0=t_blk[:, :, 0], scalar=float(P), in1=brow[:, :],
                                          op0=ALU.mult, op1=ALU.subtract))
            link(dve.tensor_scalar(btab[:, 1, :], brow[:, :], float(XR - P), None, ALU.min))
            dve.tensor_copy(btab[:, 0, :], bexp[:, :]).then_inc(btab_done, 1)
            link(dve.tensor_tensor(moved[:, :, :], sel[:, :, :, :].rearrange("p a t e -> p (a t) e"),
                                   shift[:, :].unsqueeze(1).to_broadcast([P, 2 * NT, E]), ALU.mult))
            link(dve.tensor_reduce(ypos[:, :, :].rearrange("p a t -> p (a t)"), moved[:, :, :], AX.X, ALU.add))
            link(dve.tensor_tensor(ypos[:, :, :], ypos[:, :, :], slot[:, :, :], ALU.add))
            link(dve.tensor_copy(ypos_i[:, :, :], ypos[:, :, :]))
            assert steps[0] == TABLE_OPS

            def ffn(k, j, r):
                if has(k, 2):
                    dve.wait_ge(x_hi, k + 3)
                    low_half(xT[:, j, 1, :, :], b_t[:, 0:D].rearrange("p (k s) -> p k s", k=KT), 1.0,
                             xT[:, j, 0, :, :]).then_inc(x_lo, 1)
                if has(k, 0):
                    dve.wait_ge(g_hi, k + 1)
                    low_half(gT[:, 1, :, :], b_pt[:, :].rearrange("p (k s) -> p k s", k=FT),
                             G_UP / (2 * W_UP * W_UP), gT[:, 0, :, :]).then_inc(g_lo, 1)
                if has(k, 1):
                    dve.wait_ge(tanhed, k + 2)
                    wait(dve, gg_done, k + 1)
                    dve.scalar_tensor_tensor(out=ua[:, :], in0=th[:, :], scalar=1.0, in1=b_a[(j + 1) % 2][:, :],
                                             op0=ALU.add, op1=ALU.mult).then_inc(u_done, 1)
                if has(k, 1):
                    dve.wait_ge(u_done, k + 2)
                    dve.wait_ge(b_mm, k + 2)
                    dve.tensor_tensor(gg[:, :], ua[:, :], b_s[:, :], ALU.mult).then_inc(gg_done, 1)

            all_blocks(ffn, dve)
            dve.wait_ge(gb_in, 16)
            with dve.Fori(0, NT // 4) as r:
                for k in range(4):
                    t = r * 4 + k
                    tile = bass.ds(t, 1)
                    dve.wait_ge(yg_in[k], r * 32 + 32)
                    dve.tensor_scalar(yg[:, k, 0, :], yg[:, k, 0, :], wts[:, 0, tile], None, ALU.mult) \
                        .then_inc(fin, 1)
                    dve.wait_ge(fin, r * 12 + (3 * k + 1))
                    dve.scalar_tensor_tensor(out=yg[:, k, 0, :], in0=yg[:, k, 1, :], scalar=wts[:, 1, tile],
                                             in1=yg[:, k, 0, :], op0=ALU.mult, op1=ALU.add).then_inc(fin, 1)
                    dve.wait_ge(fin, r * 12 + (3 * k + 2))
                    dve.tensor_tensor(yg[:, k, 0, :], yg[:, k, 0, :],
                                      gbB[:, bass.ds(r * 2 + k // 2, 1), :].squeeze(1), ALU.mult).then_inc(fin, 1)
                    dve.wait_ge(fin, r * 12 + (3 * k + 3))
                    dve.tensor_tensor(xs[:, tile, :].squeeze(1), xs[:, tile, :].squeeze(1), yg[:, k, 0, :],
                                      ALU.add).then_inc(fin_done, 1)

        @block.tensor
        def _(pe):
            pe.wait_ge(c_s, 2)
            pe.wait_ge(small_in, 80)
            for ps, kinds in ((b_acc, (2, 5)), (b_v, (4, 3))):
                for g, kind in enumerate(kinds):
                    for kt in range(KT):
                        m = pe.matmul(ps[0:B, g * D:(g + 1) * D], c_silu[:, kt, :],
                                      wmod_sb[:, kt, kind * D:(kind + 1) * D], start=(kt == 0), stop=(kt == KT - 1))
            m.then_inc(g_mm, 1)
            for j in range(2 * KT):
                for kt in range(KT):
                    m = pe.matmul(b_qk[:, j * B:(j + 1) * B], wmod_sb[:, kt, j * P:(j + 1) * P],
                                  c_silu[:, kt, :], start=(kt == 0), stop=(kt == KT - 1))
            m.then_inc(mod_mm, 1)
            pe.wait_ge(consts, 7)
            with pe.Fori(0, B) as b:
                pe.wait_ge(ln_z, b * TT + TT)
                for kt in range(KT):
                    for t in range(TT):
                        m = pe.transpose(b_ln[:, kt * S + t * P:kt * S + (t + 1) * P],
                                         z[:, t, kt * P:(kt + 1) * P], ident[:, :])
                m.then_inc(ln_t, 1)
                pe.wait_ge(ln_mod, b * KT + KT)
            pe.wait_ge(ln_lo, B)
            pe.wait_ge(w_lo, NCH)

            def product(out, stat, mov, n=KT):
                for q, (a, c_) in enumerate(PASSES):
                    for k in range(n):
                        m = pe.matmul(out, stat(a, k), mov(c_, k), start=(q == 0 and k == 0),
                                      stop=(q == len(PASSES) - 1 and k == n - 1))
                return m

            def tokens(b, t):
                return lambda a, k: hT[:, a, b, k, t * P:(t + 1) * P] if isinstance(b, int) else \
                    hT[:, a, bass.ds(b, 1), k, t * P:(t + 1) * P].squeeze(1)

            def weights(h, first, step, width):
                start = h * (3 * KT * DH) + first
                return lambda a, k: qkv16[:, a, bass.ds(start + k * step, width)]

            def step(i, j, b, h, g):
                if exists(i, 2):
                    pe.wait_ge(rope_done, i + 3)
                    wait(pe, t_lo, i + 2)
                    for a in range(2):
                        for t in range(TT):
                            m = pe.transpose(b_t[:, a * S + t * P:a * S + (t + 1) * P],
                                             rot[:, j % 2, (t * 2 + a) * DH:(t * 2 + a + 1) * DH], ident[:, :])
                    m.then_inc(t_mm, 1)
                if exists(i, 3):
                    bb, hh = at(i, b, h, 3)
                    wait(pe, v_lo, i + 3)
                    for t in range(TT):
                        m = product(b_v[:, t * DH:(t + 1) * DH], tokens(bb, t),
                                    weights(hh, 2 * KT * DH, DH, DH))
                    m.then_inc(v_mm, 1)
                if exists(i, 4):
                    bb, hh = at(i, b, h, 4)
                    wait(pe, rot_done, i + 4)
                    for t in range(TT):
                        m = product(b_qk[:, t * 2 * DH:(t + 1) * 2 * DH], tokens(bb, t),
                                    weights(hh, 0, 2 * DH, 2 * DH))
                    m.then_inc(qk_mm, 1)

                if exists(i, 0):
                    pe.wait_ge(pt_lo, i + 1)
                    pe.wait_ge(v_lo, i + 1)
                    wait(pe, o_lo, i)
                    product(b_pv[:, 0:S], lambda a, k: v16[:, j % 4, a, k * DH:(k + 1) * DH],
                            lambda a, k: pT[:, a, k, :]).then_inc(pv_mm, 1)
                if exists(i, 2):
                    q2 = j % 2
                    pe.wait_ge(t_lo, i + 3)
                    wait(pe, exped, i + 2)
                    for t in range(TT):
                        m = product(b_s[:, t * S:(t + 1) * S],
                                    lambda a, k: qkT[:, q2, a, t * P:(t + 1) * P],
                                    lambda a, k: qkT[:, q2, a, S:2 * S], 1)
                    m.then_inc(s_mm, 1)
                if exists(i, 1):
                    pe.wait_ge(normed, i + 2)
                    wait(pe, pt_lo, i + 1)
                    for k in range(KT):
                        for t in range(TT):
                            m = pe.transpose(b_pt[:, k * S + t * P:k * S + (t + 1) * P],
                                             ex[:, (j + 1) % 2, t, k * P:(k + 1) * P], ident[:, :])
                    m.then_inc(pt_mm, 1)
            def late(b, part):
                if part == 0:
                    pe.wait_ge(o_lo, b * H + H)
                    for t in range(TT):
                        m = product(b_acc[:, t * D:(t + 1) * D],
                                    lambda a, k: oT[:, a, k, t * P:(t + 1) * P],
                                    lambda a, k: wo16[:, a, k, :], H)
                    m.then_inc(o_mm, 1)
                if part == 2:
                    pe.wait_ge(h2_done, b * 2 + 2)
                    for kt in range(KT):
                        for t in range(TT):
                            m = pe.transpose(b_ln[:, kt * S + t * P:kt * S + (t + 1) * P],
                                             h2[:, t, kt * P:(kt + 1) * P], ident[:, :])
                    m.then_inc(h2_t, 1)
                if part == 3:
                    pe.wait_ge(h2_copy, b + 1)
                    for t in range(TT):
                        for kt in range(KT):
                            m = pe.matmul(b_ln[:, t * E:(t + 1) * E], h2T[:, kt, t * P:(t + 1) * P],
                                          gw_sb[:, kt * E:(kt + 1) * E], start=(kt == 0), stop=(kt == KT - 1))
                    m.then_inc(logit_mm, 1)
                if part == 4:
                    pe.wait_ge(rt, b * ROUTE_OPS + M16_AT)
                    for t in range(TT + 1):
                        for k in range(min(t + 1, TT)):
                            m = pe.matmul(b_ln[:, 32 + t * E:32 + (t + 1) * E],
                                          (tri16 if k == t else ones16)[:, :], m16[:, k, :],
                                          start=(k == 0), stop=(k == min(t, TT - 1)))
                    m.then_inc(rank_mm, 1)

            all_steps(step, late, pe)
            pe.wait_ge(btab_done, 1)

            last = [None]

            def expert(k):
                return pe.value_load(btab[0:1, 0, bass.ds(k, 1)], min_val=0, max_val=E - 1)

            def ffn(k, j, r):
                if has(k, 2):
                    pe.wait_ge(xg_in[j], r * 16 + 32)
                    wait(pe, x_lo, k + 2)
                    for kt in range(KT):
                        m = pe.transpose(b_t[:, kt * P:(kt + 1) * P], xg[:, j, kt * P:(kt + 1) * P], ident[:, :])
                    m.then_inc(xt_mm, 1)
                if has(k, 0):
                    pe.wait_ge(gg_done, k + 1)
                    wait(pe, g_lo, k)
                    for q in range(FT):
                        m = pe.transpose(b_pt[:, q * P:(q + 1) * P], gg[:, q * P:(q + 1) * P], ident[:, :])
                    m.then_inc(gt_mm, 1)
                stat = lambda a, q: xT[:, (j + 1) % 2, a, q, :]
                if has(k, 1):
                    e1 = expert(k + 1)
                    col = e1 * (2 * FW)
                    pe.wait_ge(w_ffn, e1 * 16 + 16)
                    pe.wait_ge(x_lo, k + 2)
                    wait(pe, u_done, k)
                    product(b_a[(j + 1) % 2][:, :], stat,
                            lambda a, q: arena[:, bass.ds(col + (a * FW + q * F), F)]).then_inc(a_mm, 1)
                if has(k, 1):
                    product(b_s[:, :], stat,
                            lambda a, q: arena[:, bass.ds(col + (a * FW + KT * F + q * F), F)]) \
                        .then_inc(b_mm, 1)
                if has(k, 0):
                    col0 = (last[0] if j == 1 and last[0] is not None else expert(k)) * (2 * FW)
                    pe.wait_ge(g_lo, k + 1)
                    wait(pe, y_out, k)
                    product(b_pv[:, 0:D], lambda a, q: gT[:, a, q, :],
                            lambda a, q: arena[:, bass.ds(col0 + (a * FW + 2 * KT * F + q * D), D)], FT) \
                        .then_inc(y_mm, 1)
                last[0] = e1 if has(k, 1) else None

            all_blocks(ffn, pe)


def kernel(**inputs):
    import numpy as np
    import concourse.bacc as bacc
    from concourse.bass_utils import run_bass_kernel_spmd as run

    a = {k: np.asarray(v) for k, v in inputs.items()}
    x = a["L0_attn_x"].reshape(T, D)
    c = a["L0_c"].T.reshape(KT, P, B).transpose(1, 0, 2).reshape(P, KT * B)
    wmod = a["L0_wmod"].reshape(KT, P, NMOD * D).transpose(1, 0, 2)
    w = a["L0_attn_w_qkv"].reshape(3, H, DH, KT, P)
    qk = w[:2].transpose(4, 1, 3, 0, 2).reshape(P, H, KT * 2 * DH)
    v = w[2].transpose(3, 0, 2, 1).reshape(P, H, KT * DH)
    wo = a["L0_attn_w_out"].reshape(D, H, DH).transpose(2, 1, 0).reshape(P, H * D)
    wall = np.concatenate([np.concatenate([qk, v], axis=2).reshape(P, WCOLS), wo], axis=1)
    inv = (1.0 / np.float32(10000.0) ** (np.arange(0, DH, 2, dtype=np.float32) / np.float32(DH))).astype(np.float32)
    ang = np.arange(S, dtype=np.float32)[:, None] * inv[None, :]
    up = float(DH) ** -0.25 / W_UP
    cos, sin = np.cos(ang) * up, np.sin(ang) * up
    cos2 = np.concatenate([cos, cos], 1).reshape(TT, P, DH)
    sin2 = np.concatenate([-sin, sin], 1).reshape(TT, P, DH)
    rope = np.stack([np.repeat(t.transpose(1, 0, 2)[:, :, None], 2, axis=2).reshape(P, TT * 2 * DH)
                     for t in (cos2, sin2)], 1).astype(np.float32)
    gate_w = a["L0_ffn_gate_w"].reshape(E, KT, P).transpose(2, 1, 0).reshape(P, KT * E)
    w1, w3 = (a[k].reshape(E, F, KT, P).transpose(0, 3, 2, 1).reshape(E, P, KT * F)
              for k in ("L0_ffn_w1", "L0_ffn_w3"))
    w2 = a["L0_ffn_w2"].reshape(E, D, FT, P).transpose(0, 3, 2, 1).reshape(E, P, FT * D)
    fw = np.concatenate([w1, w3, w2], axis=2)
    e, blk = np.arange(E), np.arange(NB)
    table = np.concatenate([np.tile(E - e, TT), e * T, np.tile(P * np.arange(NT), E),
                            np.repeat(blk, E), np.tile(e, NB)]).astype(np.float32)
    table = np.tile(table, (P, 1))
    assert table.shape == (P, TABLE)
    data = {"in_x": x, "in_c": c, "in_wmod": wmod, "in_rope": rope, "in_wall": wall,
            "in_gate_w": gate_w, "in_fw": fw, "in_table": table}
    data = {k: np.ascontiguousarray(t) for k, t in data.items()}
    nc = bacc.Bacc("TRN2", target_bir_lowering=False, num_devices=1)
    aps = [nc.dram_tensor(k, t.shape, F32, kind="ExternalInput").ap() for k, t in data.items()]
    out = nc.dram_tensor("out_x", (B, S, D), F32, kind="ExternalOutput").ap()
    scratch = [nc.dram_tensor(k, shape, dt, kind="Internal").ap() for k, shape, dt in (
        ("mod_rows", (B, 4 * D), F32), ("ffn_halves", (E, P, 2, FW), F16),
        ("expert_rows", (XR, D), F32), ("result_rows", (NB * P, D), F32))]
    build(nc, *aps, out, *scratch)
    r = run(nc, [data], core_ids=[0])
    return r.results[0]["out_x"]
```

```python
from contextlib import ExitStack

import concourse.bass as bass
from concourse import mybir

F32 = mybir.dt.float32
F16 = mybir.dt.float16
I32 = mybir.dt.int32
ALU = mybir.AluOpType
ACT = mybir.ActivationFunctionType
AX = mybir.AxisListType

P = 128
B, S, D = 8, 256, 256
H, DH = 16, 128
E, F = 8, 512
T = B * S
NT = T // P
TT = S // P
KT = D // P
NMOD = 6
EPS = 1e-5
GATE_FLOOR = 0.25

W_UP = 64.0
V_UP = 16.0
P_UP = 256.0
O_UP = 16.0
PASSES = ((0, 0), (0, 1), (1, 0))

HQ = 4
NG = H // HQ
FT = F // P
FW = 2 * KT * F + FT * D
FPART = FW // NG
NB = 2 * T // P + E - 1
XR = E * T
G_UP = 16.0
FAR = 3.0e38
JITTER = 0.02
M16_AT, EXP_AT, ROUTE_OPS, TABLE_OPS = 13, 14, 26, 24
CHAIN = {"first": 0, "second": 7, "both": 12, "kept": 15, "weights": 17, "rows": 22}
LATE = ["add", "statistics", "moments", "rstd", "normalise", "shift", "transpose", "logits",
        "first", "second", "both", "kept", "weights", "rows", "scatter 0", "scatter 1"]
PREP = {5: "normalise", 6: "transpose", 7: "modulate", 8: "low half"}
TABLE = 24 + E * NT + 2 * NB * E
WCOLS = H * 3 * KT * DH
WALL = WCOLS + H * D
NCH = 16
CH = WALL // NCH
STAGES = 4
SOON = 3


def chunks_before(i):
    if i == -HQ:
        return range(SOON)
    n = SOON + 2 * (i + HQ - 1)
    return range(n, min(n + 2, NCH)) if n < NCH else ()


def build(nc, x, c, wmod, rope, wall, gate_w, fw, table, out, mscr, wscr, xrows, yrows):
    with ExitStack() as ctx:
        def sb(name, shape, dt=F32):
            return ctx.enter_context(nc.sbuf_tensor(name, shape, dt))

        def bank(name):
            return ctx.enter_context(nc.psum_tensor(name, [P, 512], F32))

        def sem(name):
            return ctx.enter_context(nc.semaphore(name))

        arena = sb("arena", [P, E * 2 * FW], F16)
        spans = (2 * WCOLS, 2 * B * KT * S, 2 * H * D, 2 * H * S)
        assert sum(spans) == E * 2 * FW
        cuts = [sum(spans[:i]) for i in range(5)]
        qkv16 = arena[:, cuts[0]:cuts[1]].rearrange("p (a n) -> p a n", a=2)
        hT = arena[:, cuts[1]:cuts[2]].rearrange("p (a b k s) -> p a b k s", a=2, b=B, k=KT)
        wo16 = arena[:, cuts[2]:cuts[3]].rearrange("p (a h n) -> p a h n", a=2, h=H)
        oT = arena[:, cuts[3]:cuts[4]].rearrange("p (a h s) -> p a h s", a=2, h=H)
        wmod_sb = arena[:, cuts[3]:cuts[3] + 2 * KT * NMOD * D].bitcast(F32) \
            .rearrange("p (k n) -> p k n", k=KT)
        xs = sb("xs", [P, NT, D])
        stage = sb("stage", [P, STAGES, CH])
        split16 = sb("split16", [P, 2, FPART], F16)
        rope_sb = sb("rope_sb", [P, 2, TT * 2 * DH])
        c_sb = sb("c_sb", [P, KT * B])
        c_tanh = sb("c_tanh", [P, KT * B])
        c_silu = sb("c_silu", [P, KT, B])
        modT = sb("modT", [P, 2 * KT, B])
        g_sign = sb("g_sign", [B, 2 * D])
        g_abs = sb("g_abs", [B, 2 * D])
        m_row = sb("m_row", [B, 4, D])
        mB = sb("mB", [P, 4, D])
        held = sb("held", [P, 1])
        zeros = sb("zeros", [P, 512])
        stats = sb("stats", [P, NT, 6])
        mv = sb("mv", [P, NT, 2])
        rstd = sb("rstd", [P, NT])
        half_neg = sb("half_neg", [P, NT])
        z = sb("z", [P, TT, D])
        hmod = sb("hmod", [P, KT, S])
        h2 = sb("h2", [P, TT, D])
        h2T = sb("h2T", [P, KT, S])
        gw_sb = sb("gw_sb", [P, KT * E])
        ident = sb("ident", [P, P])
        qkc = sb("qkc", [P, 2, 512])
        rot = sb("rot", [P, 2, 512])
        qkT = sb("qkT", [P, 2, 2, 512], F16)
        v16 = sb("v16", [P, 4, 2, TT * DH], F16)
        ex = sb("ex", [P, 2, TT, S])
        pT = sb("pT", [P, 2, KT, S], F16)
        nmax = sb("nmax", [P, 2, TT])
        esum = sb("esum", [P, 2, TT])
        rsum = sb("rsum", [P, 2, TT])
        gated = sb("gated", [P, TT, D])
        table_sb = sb("table_sb", [P, TABLE])
        tri16 = sb("tri16", [P, P], F16)
        ones16 = sb("ones16", [P, P], F16)
        lg = sb("lg", [P, 2, TT, E])
        hit = sb("hit", [P, TT, E])
        best = sb("best", [P, TT])
        top = sb("top", [P, 2, TT])
        sel = sb("sel", [P, 2, NT, E])
        absl = sb("absl", [P, 2, TT, E])
        diff = sb("diff", [P, 2, TT, E])
        keep = sb("keep", [P, 2, TT, E])
        ediff = sb("ediff", [P, 2, TT, E])
        psum_ = sb("psum_", [P, 2, TT])
        wts = sb("wts", [P, 2, NT])
        m16 = sb("m16", [P, TT, E], F16)
        base = sb("base", [P, E])
        row = sb("row", [P, TT, E])
        srow = sb("srow", [P, 2, TT, E])
        slot = sb("slot", [P, 2, NT])
        slot_i = sb("slot_i", [P, 2, TT], I32)
        cnt = sb("cnt", [P, E])
        over = sb("over", [P, E, NT])
        ends = sb("ends", [P, 2, E])
        shift = sb("shift", [P, E])
        moved = sb("moved", [P, 2 * NT, E])
        ypos = sb("ypos", [P, 2, NT])
        ypos_i = sb("ypos_i", [P, 2, NT], I32)
        bcmp = sb("bcmp", [P, NB, E])
        bexp = sb("bexp", [P, NB])
        brow = sb("brow", [P, NB])
        btab = sb("btab", [P, 2, NB], I32)
        xg = sb("xg", [P, 2, D])
        xT = sb("xT", [P, 2, 2, KT, P], F16)
        th = sb("th", [P, F])
        ua = sb("ua", [P, F])
        gg = sb("gg", [P, F])
        gT = sb("gT", [P, 2, FT, P], F16)
        y_sb = sb("y_sb", [P, 2, D])
        yg = stage[:, 0:2, :].rearrange("p a (j n) -> p (a j) n", n=D) \
            .rearrange("p (r j) n -> p r j n", j=2)
        gbB = stage[:, 2:4, :].rearrange("p a (j n) -> p (a j) n", n=D)

        t_first = table_sb[:, 0:TT * E].rearrange("p (t e) -> p t e", e=E)
        t_base = table_sb[:, 16:24]
        t_thr = table_sb[:, 24:24 + E * NT].rearrange("p (e k) -> p e k", k=NT)
        o = 24 + E * NT
        t_blk = table_sb[:, o:o + NB * E].rearrange("p (k e) -> p k e", e=E)
        t_exp = table_sb[:, o + NB * E:o + 2 * NB * E].rearrange("p (k e) -> p k e", e=E)

        b_qk, b_v, b_t, b_pt, b_s, b_pv, b_acc, b_ln = (
            bank(n) for n in ("b_qk", "b_v", "b_t", "b_pt", "b_s", "b_pv", "b_acc", "b_ln"))

        b_a = (b_qk, b_v)

        x_in, x_rest_in, small_in, w_in = sem("x_in"), sem("x_rest_in"), sem("small_in"), [sem(f"w_in{i}") for i in range(STAGES)]
        w_hi, w_lo = sem("w_hi"), sem("w_lo")
        consts = sem("consts")
        c_t, c_s = sem("c_t"), sem("c_s")
        c_in, wmod_in, rope_in, mod_done = (sem(n) for n in ("c_in", "wmod_in", "rope_in", "mod_done"))
        mod_mm, mod_sb, g_mm, g_done, g_out, m_in = (
            sem(n) for n in ("mod_mm", "mod_sb", "g_mm", "g_done", "g_out", "m_in"))
        ln_stat, ln_mv, ln_rstd, ln_z, ln_t, ln_hi, ln_mod, ln_lo = (
            sem(n) for n in ("ln_stat", "ln_mv", "ln_rstd", "ln_z", "ln_t", "ln_hi", "ln_mod", "ln_lo"))
        qk_mm, v_mm, t_mm, s_mm, pt_mm, pv_mm, o_mm = (
            sem(n) for n in ("qk_mm", "v_mm", "t_mm", "s_mm", "pt_mm", "pv_mm", "o_mm"))
        qk_copied, v_hi, t_hi, exped, pt_hi, o_hi = (
            sem(n) for n in ("qk_copied", "v_hi", "t_hi", "exped", "pt_hi", "o_hi"))
        rot_done, v_lo, t_lo, maxed, rsummed, pt_lo, o_lo, gate_done, x1_done = (
            sem(n) for n in ("rot_done", "v_lo", "t_lo", "maxed", "rsummed", "pt_lo", "o_lo",
                             "gate_done", "x1_done"))
        cos_done, rope_done, normed = sem("cos_done"), sem("rope_done"), sem("normed")
        fw_in, fw_hi, fw_lo, fw_out, w_ffn = (sem(n) for n in ("fw_in", "fw_hi", "fw_lo", "fw_out", "w_ffn"))
        l2_stat, l2_mv, l2_rstd, l2_z, h2_done, h2_t, h2_copy, logit_mm, rt, rt_exp, rank_mm = (
            sem(n) for n in ("l2_stat", "l2_mv", "l2_rstd", "l2_z", "h2_done", "h2_t", "h2_copy",
                             "logit_mm", "rt", "rt_exp", "rank_mm"))
        scattered, bt, btab_done = sem("scattered"), sem("bt"), sem("btab_done")
        xg_in = [sem(f"xg_in{i}") for i in range(2)]
        y_st = [sem(f"y_st{i}") for i in range(2)]
        xt_mm, a_mm, gt_mm, b_mm, y_mm = (sem(n) for n in ("xt_mm", "a_mm", "gt_mm", "b_mm", "y_mm"))
        x_hi, tanhed, g_hi, y_out = (sem(n) for n in ("x_hi", "tanhed", "g_hi", "y_out"))
        x_lo, u_done, g_lo, gg_done = (sem(n) for n in ("x_lo", "u_done", "g_lo", "gg_done"))
        yg_in = [sem(f"yg_in{i}") for i in range(4)]
        gb_in, fin, fin_done, stored = sem("gb_in"), sem("fin"), sem("fin_done"), sem("stored")

        block = ctx.enter_context(nc.Block())

        def batch_steps(n, step, late, prep, first=None):
            if late:
                late(n - 1, "project")
            for g in range(NG):
                for j in range(HQ):
                    if first:
                        first(g * HQ + j)
                    step(n * H + (g * HQ + j), j, n, g * HQ + j, g)
                    if late:
                        late(n - 1, LATE[g * HQ + j])
                    if prep and g * HQ + j in PREP:
                        prep(n + 1, PREP[g * HQ + j])

        def run_heads(step, late, prep, first, eng):
            for piece in PREP.values():
                prep(0, piece)
            for i in range(-HQ, 0):
                first(i)
                step(i, i % HQ, 0, i, 0)
            batch_steps(0, step, None, prep, first)
            with eng.Fori(1, B - 1) as n:
                batch_steps(n, step, late, prep)
            batch_steps(B - 1, step, late, None)
            for piece in ["project"] + LATE:
                late(B - 1, piece)

        def head_out(half, h):
            return oT[:, half, h, :]

        def weights_chunk(half, n):
            if n * CH < WCOLS:
                return qkv16[:, half, n * CH:(n + 1) * CH]
            first = (n * CH - WCOLS) // D
            return wo16[:, half, first:first + CH // D, :].rearrange("p h n -> p (h n)")

        def exists(i, ahead):
            return not isinstance(i, int) or 0 <= i + ahead < B * H

        def at(i, b, h, ahead):
            if isinstance(i, int):
                return divmod(i + ahead, H)
            if h + ahead < H:
                return b, h + ahead
            return b + 1, h + ahead - H

        def wait(eng, s, value):
            if not (isinstance(value, int) and value <= 0):
                eng.wait_ge(s, value)

        def all_blocks(step, eng):
            for k in range(-2, 2):
                step(k, k % 2, (k - k % 2) // 2)
            with eng.Fori(1, (NB - 5) // 2) as r:
                for j in range(2):
                    step(r * 2 + j, j, r)
            for k in range((NB - 5) // 2 * 2, NB):
                step(k, k % 2, k // 2)

        def has(k, ahead):
            return not isinstance(k, int) or 0 <= k + ahead < NB

        @block.sync
        def _(sp):
            xt = x.rearrange("(t p) n -> p t n", p=P)
            sp.dma_start(xs[:, 0:TT, :], xt[:, 0:TT, :]).then_inc(x_in, 16)
            for k in range(STAGES):
                sp.dma_start(stage[:, k, :], wall[:, k * CH:(k + 1) * CH]).then_inc(w_in[k], 16)
            sp.dma_start(xs[:, TT:NT, :], xt[:, TT:NT, :]).then_inc(x_rest_in, 16)
            for k in range(STAGES, NCH):
                sp.wait_ge(w_lo, k + 1 - STAGES)
                sp.dma_start(stage[:, k % STAGES, :], wall[:, k * CH:(k + 1) * CH]) \
                    .then_inc(w_in[k % STAGES], 16)
                if k == NCH // 2:
                    sp.wait_ge(g_done, 3)
                    sp.dma_start(mscr, m_row[:, :, :].rearrange("b k n -> b (k n)")).then_inc(g_out, 16)
            sp.wait_ge(w_lo, NCH - STAGES + 1)
            sp.dma_start(stage[:, 0, 0:FPART], fw[0, :, 0:FPART]).then_inc(fw_in, 16)
            sp.wait_ge(g_out, 16)
            sp.dma_start(mB[:, :, :], mscr[0:1, :].partition_broadcast(P)).then_inc(m_in, 16)

            def part_out(b, g):
                sp.wait_ge(fw_lo, b * NG + (g + 1))
                dst = wscr[b, :, :, g * FPART:(g + 1) * FPART] if isinstance(b, int) else \
                    wscr[bass.ds(b, 1), :, :, g * FPART:(g + 1) * FPART].squeeze(0)
                sp.dma_start(dst, split16[:, :, :]).then_inc(fw_out, 16)

            def part_in(b, g):
                src = fw[b, :, g * FPART:(g + 1) * FPART] if isinstance(b, int) else \
                    fw[bass.ds(b, 1), :, g * FPART:(g + 1) * FPART].squeeze(0)
                sp.dma_start(stage[:, 0, 0:FPART], src).then_inc(fw_in, 16)

            def next_part(b, g):
                part_out(b, g)
                if isinstance(g, int) and g + 1 < NG:
                    part_in(b, g + 1)
                elif not isinstance(b, int):
                    part_in(b + 1, 0)

            next_part(0, 0)
            next_part(0, 1)
            with sp.Fori(1, B) as b:
                next_part(b - 1, 2)
                next_part(b - 1, 3)
                next_part(b, 0)
                next_part(b, 1)
                sp.wait_ge(h2_done, b * 2)
                sp.dma_start(mB[:, :, :], mscr[bass.ds(b, 1), :].partition_broadcast(P)).then_inc(m_in, 16)
            next_part(B - 1, 2)
            next_part(B - 1, 3)
            sp.wait_ge(fw_out, 16 * B * NG)
            sp.wait_ge(v_mm, B * H)
            sp.wait_ge(qk_mm, B * H)
            for e in range(E):
                if e * 2 * FW + 2 * FW > cuts[2]:
                    sp.wait_ge(o_mm, B)
                sp.dma_start(arena[:, e * 2 * FW:(e + 1) * 2 * FW],
                             wscr[e].rearrange("p a n -> p (a n)")).then_inc(w_ffn, 16)
                sp.wait_ge(w_ffn, 16 * (e + 1))
            sp.dma_start(gbB, mscr[:, D:2 * D].unsqueeze(0).partition_broadcast(P)).then_inc(gb_in, 16)
            for b in range(B):
                sp.wait_ge(fin_done, (b + 1) * TT)
                sp.dma_start(out[b].rearrange("(t p) n -> p t n", p=P), xs[:, b * TT:(b + 1) * TT, :]) \
                    .then_inc(stored, 16)
            sp.wait_ge(stored, 16 * B)

        @block.gpsimd
        def _(pool):
            pool.memset(ident[:, :], 0.0).then_inc(consts, 1)
            pool.memset(tri16[:, :], 1.0).then_inc(consts, 1)
            pool.memset(half_neg[:, :], -0.5).then_inc(consts, 1)
            pool.memset(zeros[:, :], 0.0).then_inc(consts, 1)
            pool.memset(ones16[:, :], 1.0).then_inc(consts, 1)
            pool.wait_ge(consts, 5)
            pool.affine_select(out=ident[:, :], in_=ident[:, :], compare_op=ALU.not_equal, fill=1.0,
                               base=0, pattern=[[-1, P]], channel_multiplier=1).then_inc(consts, 1)
            pool.affine_select(out=tri16[:, :], in_=tri16[:, :], compare_op=ALU.is_gt, fill=0.0,
                               base=0, pattern=[[1, P]], channel_multiplier=-1).then_inc(consts, 1)
            pool.wait_ge(ln_mv, TT + 1)
            pool.tensor_tensor(rstd[:, 0:TT], mv[:, 0:TT, 1], half_neg[:, 0:TT], ALU.pow).then_inc(ln_rstd, 1)

            pool.wait_ge(rope_in, 16)

            def first(i):
                if i == 0:
                    pool.wait_ge(ln_mv, NT + 2)
                    pool.tensor_tensor(rstd[:, TT:NT], mv[:, TT:NT, 1], half_neg[:, TT:NT], ALU.pow) \
                        .then_inc(ln_rstd, 1)
                if i // 4 == 1:
                    q, n = i % 4, XR // P * D // 4
                    xflat = xrows.rearrange("(p r) n -> p (r n)", p=P)
                    pool.dma_start(xflat[:, q * n:(q + 1) * n].rearrange("p (r n) -> p r n", n=512),
                                   zeros[:, :].unsqueeze(1).to_broadcast([P, n // 512, 512])) \
                        .then_inc(scattered, 16)

            def prep(b, piece):
                if piece == "low half":
                    pool.wait_ge(ln_mod, b * KT + KT)
                    pool.tensor_tensor(hT[:, 1, bass.ds(b, 1), :, :].squeeze(1), hmod[:, :, :],
                                       hT[:, 0, bass.ds(b, 1), :, :].squeeze(1), ALU.subtract) \
                        .then_inc(ln_lo, 1)

            def step(i, j, b, h, g):
                if exists(i, 4):
                    k = j % 2
                    pool.wait_ge(qk_copied, i + 5)
                    pool.tensor_tensor(qkc[:, k, :], qkc[:, k, :], rope_sb[:, 0, :], ALU.mult) \
                        .then_inc(cos_done, 1)
                    pool.wait_ge(cos_done, i + 5)
                    pool.wait_ge(rot_done, i + 5)
                    pool.tensor_tensor(rot[:, k, :], qkc[:, k, :], rot[:, k, :], ALU.add) \
                        .then_inc(rope_done, 1)
                if exists(i, 2):
                    e = ex[:, (j + 2) % 2, :, :]
                    pool.wait_ge(rsummed, i + 3)
                    pool.tensor_tensor(e, e, rsum[:, (j + 2) % 2, :].unsqueeze(2).to_broadcast([P, TT, S]),
                                       ALU.mult).then_inc(normed, 1)

            def late(b, piece):
                if piece == "rstd":
                    pool.wait_ge(l2_mv, (b + 1) * (TT + 1))
                    pool.tensor_tensor(rstd[:, 0:TT], mv[:, 0:TT, 1], half_neg[:, 0:TT], ALU.pow) \
                        .then_inc(l2_rstd, 1)
                if piece == "normalise":
                    pool.wait_ge(scattered, (b + 1) * 64)
                    pool.wait_ge(l2_z, (b + 1) * TT)
                    pool.wait_ge(m_in, (b + 1) * 16)
                    pool.tensor_tensor(h2[:, :, :], z[:, :, :], mB[:, 2:3, :].to_broadcast([P, TT, D]),
                                       ALU.mult).then_inc(h2_done, 1)
                if piece == "shift":
                    pool.wait_ge(h2_done, b * 2 + 1)
                    pool.tensor_tensor(h2[:, :, :], h2[:, :, :], mB[:, 3:4, :].to_broadcast([P, TT, D]),
                                       ALU.add).then_inc(h2_done, 1)
                if piece == "scatter 0":
                    pool.wait_ge(rt, (b + 1) * ROUTE_OPS)
                    pool.tensor_tensor(held[:, :], half_neg[:, 0:1], half_neg[:, 1:2], ALU.mult)
                if piece in ("scatter 0", "scatter 1"):
                    q = int(piece[-1])
                    for t in range(TT):
                        pool.indirect_dma_start(
                            xrows, bass.IndirectOffsetOnAxis(ap=slot_i[:, q, t:t + 1], axis=0),
                            h2[:, t, :], None).then_inc(scattered, 16)

            run_heads(step, late, prep, first, pool)

            def put(k, j, r):
                if has(k, 0):
                    pool.wait_ge(y_out, k + 1)
                    pool.dma_start(yrows[bass.ds(k * P, P), :], y_sb[:, j, :]).then_inc(y_st[j], 16)

            all_blocks(put, pool)
            for j in range(2):
                pool.wait_ge(y_st[j], 16 * ((NB + 1 - j) // 2))
            pool.wait_ge(bt, TABLE_OPS)

            def gather(t, k):
                for q in range(2):
                    pool.indirect_dma_start(
                        yg[:, k, q, :], None, yrows,
                        bass.IndirectOffsetOnAxis(ap=ypos_i[:, q, t:t + 1], axis=0)) \
                        .then_inc(yg_in[k], 16)

            for k in range(4):
                gather(k, k)
            for t in range(4, NT):
                pool.wait_ge(fin_done, t - 3)
                gather(t, t % 4)

        @block.scalar
        def _(act):
            act.dma_start(c_sb[:, :], c).then_inc(c_in, 16)
            act.dma_start(wmod_sb, wmod).then_inc(wmod_in, 16)
            act.dma_start(rope_sb[:, :, :], rope).then_inc(rope_in, 16)
            act.dma_start(gw_sb[:, :], gate_w).then_inc(small_in, 16)
            act.dma_start(table_sb[:, :], table).then_inc(small_in, 16)
            act.wait_ge(c_in, 16)
            act.activation(c_tanh[:, :], c_sb[:, :], ACT.Tanh, scale=0.5).then_inc(c_t, 1)

            def first(i):
                for n in chunks_before(i):
                    act.wait_ge(w_in[n % STAGES], n // STAGES * 16 + 16)
                    act.activation(weights_chunk(0, n), stage[:, n % STAGES, :], ACT.Copy, scale=W_UP) \
                        .then_inc(w_hi, 1)

            def prep(b, piece):
                if piece == "transpose":
                    act.wait_ge(mod_done, 2)
                    act.wait_ge(ln_t, b + 1)
                    for kt in range(KT):
                        act.activation(hT[:, 0, bass.ds(b, 1), kt, :].squeeze(1), b_acc[:, kt * S:(kt + 1) * S],
                                       ACT.Identity, bias=modT[:, kt, bass.ds(b, 1)],
                                       scale=modT[:, KT + kt, bass.ds(b, 1)]).then_inc(ln_hi, 1)

            def step(i, j, b, h, g):
                if exists(i, 2):
                    act.wait_ge(t_mm, i + 3)
                    wait(act, s_mm, i + 1)
                    act.activation(qkT[:, j % 2, 0, :], b_t[:, :], ACT.Copy).then_inc(t_hi, 1)
                if exists(i, 3):
                    act.wait_ge(v_mm, i + 4)
                    wait(act, pv_mm, i)
                    act.activation(v16[:, (j + 3) % 4, 0, :], b_v[:, 0:TT * DH], ACT.Copy,
                                   scale=V_UP / W_UP).then_inc(v_hi, 1)
                if exists(i, 4):
                    act.wait_ge(qk_mm, i + 5)
                    wait(act, rope_done, i + 3)
                    act.activation(qkc[:, j % 2, :], b_qk[:, :], ACT.Copy).then_inc(qk_copied, 1)
                if exists(i, 0):
                    act.wait_ge(pv_mm, i + 1)
                    act.activation(head_out(0, h), b_pv[:, 0:S], ACT.Copy,
                                   scale=O_UP / (P_UP * V_UP)).then_inc(o_hi, 1)
                if exists(i, 1):
                    act.wait_ge(pt_mm, i + 2)
                    wait(act, pv_mm, i + 1)
                    act.activation(pT[:, 0, :, :], b_pt[:, :].rearrange("p (k s) -> p k s", k=KT),
                                   ACT.Copy, scale=P_UP).then_inc(pt_hi, 1)
                if exists(i, 2):
                    k = j % 2
                    act.wait_ge(maxed, i + 3)
                    wait(act, pt_mm, i + 1)
                    wait(act, rsummed, i + 1)
                    for t in range(TT):
                        e = act.activation(ex[:, k, t, :], b_s[:, t * S:(t + 1) * S], ACT.Exp,
                                           bias=nmax[:, k, t:t + 1], accum_out=esum[:, k, t:t + 1])
                    e.then_inc(exped, 1)
                if j == HQ - 1 and exists(i, 0):
                    part = b * NG + g
                    act.wait_ge(fw_in, part * 16 + 16)
                    wait(act, fw_out, part * 16)
                    act.activation(split16[:, 0, :], stage[:, 0, 0:FPART], ACT.Copy, scale=W_UP) \
                        .then_inc(fw_hi, 1)

            def late(b, piece):
                if piece == "transpose":
                    act.wait_ge(h2_t, b + 1)
                    act.activation(h2T[:, :, :], b_ln[:, :].rearrange("p (k s) -> p k s", k=KT), ACT.Copy) \
                        .then_inc(h2_copy, 1)
                if piece == "kept":
                    act.wait_ge(rt, b * ROUTE_OPS + EXP_AT)
                    act.activation(ediff[:, :, :, :], diff[:, :, :, :], ACT.Exp).then_inc(rt_exp, 1)

            run_heads(step, late, prep, first, act)
            act.wait_ge(btab_done, 1)
            act.wait_ge(scattered, (B + 1) * 64)

            def get(k, slot):
                start = act.value_load(btab[0:1, 1, bass.ds(k, 1)], min_val=0, max_val=XR - P)
                act.dma_start(xg[:, slot, :], xrows[bass.ds(start, P), :]).then_inc(xg_in[slot], 16)

            get(0, 0)
            get(1, 1)

            def ffn(k, j, r):
                if has(k, 2):
                    act.wait_ge(xt_mm, k + 3)
                    wait(act, b_mm, k + 1)
                    act.activation(xT[:, j, 0, :, :], b_t[:, 0:D].rearrange("p (k s) -> p k s", k=KT),
                                   ACT.Copy).then_inc(x_hi, 1)
                if has(k, 4):
                    get(k + 4, j)
                if has(k, 0):
                    act.wait_ge(gt_mm, k + 1)
                    wait(act, y_mm, k)
                    act.activation(gT[:, 0, :, :], b_pt[:, :].rearrange("p (k s) -> p k s", k=FT), ACT.Copy,
                                   scale=G_UP / (2 * W_UP * W_UP)).then_inc(g_hi, 1)
                if has(k, 1):
                    act.wait_ge(a_mm, k + 2)
                    wait(act, u_done, k + 1)
                    act.activation(th[:, :], b_a[(j + 1) % 2][:, :], ACT.Tanh, scale=0.5 / W_UP) \
                        .then_inc(tanhed, 1)
                if has(k, 0):
                    act.wait_ge(y_mm, k + 1)
                    wait(act, y_st[j], r * 16)
                    act.activation(y_sb[:, j, :], b_pv[:, 0:D], ACT.Copy).then_inc(y_out, 1)

            all_blocks(ffn, act)

        @block.vector
        def _(dve):
            def low_half(out, full, scale, hi):
                return dve.scalar_tensor_tensor(out=out, in0=full, scalar=scale, in1=hi,
                                                op0=ALU.mult, op1=ALU.subtract)

            def statistics(a, b):
                before = dve_stats[0]
                for t in range(a, b):
                    dve.bn_stats(stats[:, t, :], xs[:, t, :]).then_inc(ln_stat, 1)
                dve.wait_ge(ln_stat, b)
                for t in range(a, b):
                    dve.bn_aggr(mv[:, t, :], stats[:, t, :]).then_inc(ln_mv, 1)
                dve.wait_ge(ln_mv, before + b - a)
                dve.tensor_scalar(mv[:, a:b, 1], mv[:, a:b, 1], EPS, None, ALU.add).then_inc(ln_mv, 1)
                dve_stats[0] += b - a + 1

            dve_stats = [0]
            dve.wait_ge(x_in, 16)
            statistics(0, TT)
            dve.wait_ge(c_t, 1)
            dve.wait_ge(c_in, 16)
            dve.scalar_tensor_tensor(out=c_tanh[:, :], in0=c_tanh[:, :], scalar=1.0, in1=c_sb[:, :],
                                     op0=ALU.add, op1=ALU.mult).then_inc(c_s, 1)
            dve.wait_ge(c_s, 1)
            dve.tensor_scalar(c_silu[:, :, :], c_tanh[:, :].rearrange("p (k b) -> p k b", k=KT), 0.5, None,
                              ALU.mult).then_inc(c_s, 1)
            mod_ps = b_qk[:, 0:2 * KT * B].rearrange("p (m b) -> p m b", b=B)

            def prep(b, piece):
                if piece == "normalise":
                    if isinstance(b, int):
                        dve.wait_ge(ln_rstd, min(b, 1) + 1)
                    else:
                        dve.wait_ge(h2_done, b * 2 - 3)
                    for t in range(TT):
                        tile = bass.ds(b * TT + t, 1)
                        dve.tensor_scalar(z[:, t, :], xs[:, tile, :].squeeze(1),
                                          mv[:, tile, 0:1].squeeze(1), rstd[:, tile],
                                          ALU.subtract, ALU.mult).then_inc(ln_z, 1)
                    if isinstance(b, int) and b == 0:
                        dve.wait_ge(mod_mm, 1)
                        dve.tensor_copy(modT[:, 0:KT, :], mod_ps[:, 0:KT, :]).then_inc(mod_done, 1)
                        dve.tensor_scalar(modT[:, KT:2 * KT, :], mod_ps[:, KT:2 * KT, :], 1.0, None, ALU.add) \
                            .then_inc(mod_done, 1)
                        dve.wait_ge(mod_done, 2)
                        dve.wait_ge(rope_in, 16)
                if piece == "modulate":
                    dve.wait_ge(ln_hi, b * KT + KT)
                    for kt in range(KT):
                        dve.tensor_scalar(hmod[:, kt, :], b_acc[:, kt * S:(kt + 1) * S],
                                          modT[:, KT + kt, bass.ds(b, 1)], modT[:, kt, bass.ds(b, 1)],
                                          ALU.mult, ALU.add).then_inc(ln_mod, 1)

            def first(i):
                for n in chunks_before(i):
                    dve.wait_ge(w_hi, n + 1)
                    low_half(weights_chunk(1, n), stage[:, n % STAGES, :], W_UP, weights_chunk(0, n)) \
                        .then_inc(w_lo, 1)
                if i == -2:
                    assert O_UP == G_UP
                    unit = 1.0 / (W_UP * O_UP)
                    dve.wait_ge(g_mm, 1)
                    dve.tensor_scalar(g_sign[:, :], b_ln[0:B, :], 0.0, 2.0 * unit, ALU.is_ge, ALU.mult) \
                        .then_inc(mod_sb, 1)
                    dve.tensor_scalar(g_abs[:, :], b_ln[0:B, :], -1.0, GATE_FLOOR, ALU.mult, ALU.max) \
                        .then_inc(mod_sb, 1)
                    dve.wait_ge(mod_sb, 2)
                    dve.tensor_tensor(g_abs[:, :], b_ln[0:B, :], g_abs[:, :], ALU.max).then_inc(mod_sb, 1)
                    dve.wait_ge(mod_sb, 3)
                    dve.scalar_tensor_tensor(out=m_row[:, 0:2, :], in0=g_sign[:, :].rearrange("b (k n) -> b k n", k=2),
                                             scalar=-unit, in1=g_abs[:, :].rearrange("b (k n) -> b k n", k=2),
                                             op0=ALU.add, op1=ALU.mult).then_inc(g_done, 1)
                    dve.tensor_scalar(m_row[:, 2, :], b_pv[0:B, 0:D], 1.0, None, ALU.add).then_inc(g_done, 1)
                    dve.tensor_copy(m_row[:, 3, :], b_pv[0:B, D:2 * D]).then_inc(g_done, 1)
                if i == -1:
                    dve.wait_ge(small_in, 32)
                    dve.tensor_copy(base[:, :], t_base)
                    dve.wait_ge(x_rest_in, 16)
                    statistics(TT, NT)

            qk4 = b_qk[:, :].rearrange("p (a f d) -> p a f d", a=TT * 2, f=2)

            def step(i, j, b, h, g):
                if exists(i, 2):
                    dve.wait_ge(t_hi, i + 3)
                    low_half(qkT[:, j % 2, 1, :], b_t[:, :], 1.0, qkT[:, j % 2, 0, :]).then_inc(t_lo, 1)
                if exists(i, 3):
                    k = (j + 3) % 4
                    dve.wait_ge(v_hi, i + 4)
                    low_half(v16[:, k, 1, :], b_v[:, 0:TT * DH], V_UP / W_UP, v16[:, k, 0, :]) \
                        .then_inc(v_lo, 1)
                if exists(i, 4):
                    k = j % 2
                    dve.wait_ge(qk_copied, i + 5)
                    wait(dve, t_mm, i + 3)
                    r4 = rot[:, k, :].rearrange("p (a f d) -> p a f d", a=TT * 2, f=2)
                    s4 = rope_sb[:, 1, :].rearrange("p (a f d) -> p a f d", a=TT * 2, f=2)
                    dve.tensor_tensor(r4[:, :, 0, :], qk4[:, :, 1, :], s4[:, :, 0, :], ALU.mult)
                    dve.tensor_tensor(r4[:, :, 1, :], qk4[:, :, 0, :], s4[:, :, 1, :], ALU.mult) \
                        .then_inc(rot_done, 1)
                if exists(i, 0):
                    dve.wait_ge(o_hi, i + 1)
                    low_half(head_out(1, h), b_pv[:, 0:S], O_UP / (P_UP * V_UP), head_out(0, h)) \
                        .then_inc(o_lo, 1)
                if exists(i, 2):
                    dve.wait_ge(s_mm, i + 3)
                    wait(dve, exped, i + 1)
                    dve.tensor_reduce(nmax[:, j % 2, :], b_s[:, :].rearrange("p (t s) -> p t s", t=TT),
                                      AX.X, ALU.max, negate=True).then_inc(maxed, 1)
                if exists(i, 1):
                    dve.wait_ge(pt_hi, i + 2)
                    low_half(pT[:, 1, :, :], b_pt[:, :].rearrange("p (k s) -> p k s", k=KT), P_UP,
                             pT[:, 0, :, :]).then_inc(pt_lo, 1)
                if exists(i, 2):
                    dve.wait_ge(exped, i + 3)
                    wait(dve, normed, i + 1)
                    dve.reciprocal(rsum[:, j % 2, :], esum[:, j % 2, :]).then_inc(rsummed, 1)
                if j == HQ - 1 and exists(i, 0):
                    dve.wait_ge(fw_hi, b * NG + g + 1)
                    low_half(split16[:, 1, :], stage[:, 0, 0:FPART], W_UP, split16[:, 0, :]) \
                        .then_inc(fw_lo, 1)

            def late(b, piece):
                tiles = bass.ds(b * TT, TT)
                done = [CHAIN.get(piece, 0)]

                def link(ins):
                    done[0] += 1
                    ins.then_inc(rt, 1)
                    dve.wait_ge(rt, b * ROUTE_OPS + done[0])

                if piece == "add":
                    dve.wait_ge(o_mm, b + 1)
                    dve.wait_ge(m_in, (b + 1) * 16)
                    dve.tensor_tensor(gated[:, :, :], b_acc[:, :].rearrange("p (t n) -> p t n", t=TT),
                                      mB[:, 0:1, :].to_broadcast([P, TT, D]), ALU.mult) \
                        .then_inc(gate_done, 1)
                    dve.wait_ge(gate_done, b + 1)
                    dve.tensor_tensor(z[:, :, :], xs[:, tiles, :], gated[:, :, :], ALU.add) \
                        .then_inc(x1_done, 1)
                if piece == "statistics":
                    dve.wait_ge(x1_done, b + 1)
                    for t in range(TT):
                        dve.bn_stats(stats[:, t, :], z[:, t, :]).then_inc(l2_stat, 1)
                if piece == "moments":
                    dve.wait_ge(l2_stat, (b + 1) * TT)
                    dve.tensor_tensor(xs[:, tiles, :], xs[:, tiles, :], gated[:, :, :], ALU.add)
                    for t in range(TT):
                        dve.bn_aggr(mv[:, t, :], stats[:, t, :]).then_inc(l2_mv, 1)
                    dve.wait_ge(l2_mv, b * (TT + 1) + TT)
                    dve.tensor_scalar(mv[:, 0:TT, 1], mv[:, 0:TT, 1], EPS, None, ALU.add).then_inc(l2_mv, 1)
                if piece == "normalise":
                    dve.wait_ge(l2_rstd, b + 1)
                    for t in range(TT):
                        dve.tensor_scalar(z[:, t, :], z[:, t, :], mv[:, t, 0:1], rstd[:, t:t + 1],
                                          ALU.subtract, ALU.mult).then_inc(l2_z, 1)
                if piece == "first":
                    dve.wait_ge(logit_mm, b + 1)
                    link(dve.tensor_copy(lg[:, 0, :, :], b_ln[:, 0:TT * E].rearrange("p (t e) -> p t e", e=E)))
                if piece in ("first", "second"):
                    q = ("first", "second").index(piece)
                    link(dve.tensor_reduce(top[:, q, :], lg[:, q, :, :], AX.X, ALU.max))
                    link(dve.tensor_tensor(hit[:, :, :], lg[:, q, :, :],
                                           top[:, q, :].unsqueeze(2).to_broadcast([P, TT, E]), ALU.is_equal))
                    link(dve.tensor_tensor(hit[:, :, :], hit[:, :, :], t_first, ALU.mult))
                    link(dve.tensor_reduce(best[:, :], hit[:, :, :], AX.X, ALU.max))
                    link(dve.tensor_tensor(sel[:, q, tiles, :], hit[:, :, :],
                                           best[:, :].unsqueeze(2).to_broadcast([P, TT, E]), ALU.is_equal))
                if piece == "first":
                    link(dve.scalar_tensor_tensor(out=lg[:, 1, :, :], in0=sel[:, 0, tiles, :], scalar=-FAR,
                                                  in1=lg[:, 0, :, :], op0=ALU.mult, op1=ALU.add))
                topb = top[:, :, :].unsqueeze(3).to_broadcast([P, 2, TT, E])
                if piece == "both":
                    link(dve.tensor_tensor(m16[:, :, :], sel[:, 0, tiles, :], sel[:, 1, tiles, :], ALU.add))
                    assert done[0] == M16_AT
                    link(dve.tensor_tensor(diff[:, :, :, :], lg[:, :, :, :], topb, ALU.subtract))
                    assert done[0] == EXP_AT
                    link(dve.scalar_tensor_tensor(out=absl[:, :, :, :], in0=lg[:, :, :, :], scalar=-1.0,
                                                  in1=lg[:, :, :, :], op0=ALU.mult, op1=ALU.max))
                if piece == "kept":
                    link(dve.tensor_tensor(absl[:, :, :, :], absl[:, :, :, :], topb, ALU.max))
                    link(dve.scalar_tensor_tensor(out=keep[:, :, :, :], in0=absl[:, :, :, :], scalar=-JITTER,
                                                  in1=diff[:, :, :, :], op0=ALU.mult, op1=ALU.is_le))
                ranks = b_ln[:, 32:32 + (TT + 1) * E].rearrange("p (t e) -> p t e", e=E)
                if piece == "weights":
                    dve.wait_ge(rt_exp, b + 1)
                    link(dve.tensor_tensor(keep[:, :, :, :], keep[:, :, :, :], ediff[:, :, :, :], ALU.mult))
                    link(dve.tensor_reduce(psum_[:, :, :], keep[:, :, :, :], AX.X, ALU.add))
                    link(dve.reciprocal(wts[:, :, tiles], psum_[:, :, :]))
                    dve.wait_ge(rank_mm, b + 1)
                    link(dve.tensor_tensor(row[:, :, :], ranks[:, 0:TT, :],
                                           base[:, :].unsqueeze(1).to_broadcast([P, TT, E]), ALU.add))
                    link(dve.tensor_tensor(base[:, :], base[:, :], ranks[:, TT, :], ALU.add))
                if piece == "rows":
                    for q in range(2):
                        link(dve.tensor_tensor(srow[:, q, :, :], sel[:, q, tiles, :], row[:, :, :], ALU.mult))
                    link(dve.tensor_reduce(slot[:, :, tiles], srow[:, :, :, :], AX.X, ALU.add))
                    link(dve.tensor_scalar(slot_i[:, :, :], slot[:, :, tiles], 1.0, None, ALU.mult))
                    assert done[0] == ROUTE_OPS

            run_heads(step, late, prep, first, dve)

            steps = [0]

            def link(ins):
                steps[0] += 1
                ins.then_inc(bt, 1)
                dve.wait_ge(bt, steps[0])

            def over_blocks(v):
                return v.unsqueeze(1).to_broadcast([P, NB, E])

            link(dve.tensor_tensor(cnt[:, :], base[:, :], t_base, ALU.subtract))
            link(dve.tensor_tensor(over[:, :, :], cnt[:, :].unsqueeze(2).to_broadcast([P, E, NT]), t_thr,
                                   ALU.is_gt))
            link(dve.tensor_reduce(cnt[:, :], over[:, :, :], AX.X, ALU.add))
            link(dve.tensor_copy(ends[:, 0, :], cnt[:, :]))
            q = 0
            for d in (1, 2, 4):
                link(dve.tensor_copy(ends[:, 1 - q, 0:d], ends[:, q, 0:d]))
                link(dve.tensor_tensor(ends[:, 1 - q, d:E], ends[:, q, d:E], ends[:, q, 0:E - d], ALU.add))
                q = 1 - q
            link(dve.tensor_tensor(shift[:, :], ends[:, q, :], cnt[:, :], ALU.subtract))
            link(dve.scalar_tensor_tensor(out=shift[:, :], in0=shift[:, :], scalar=float(P), in1=t_base,
                                          op0=ALU.mult, op1=ALU.subtract))
            link(dve.tensor_tensor(bcmp[:, :, :], t_blk, over_blocks(ends[:, q, :]), ALU.is_ge))
            link(dve.tensor_reduce(bexp[:, :], bcmp[:, :, :], AX.X, ALU.add))
            link(dve.tensor_scalar(bexp[:, :], bexp[:, :], E - 1.0, None, ALU.min))
            link(dve.tensor_tensor(bcmp[:, :, :], t_exp, bexp[:, :].unsqueeze(2).to_broadcast([P, NB, E]),
                                   ALU.is_equal))
            link(dve.tensor_tensor(bcmp[:, :, :], bcmp[:, :, :], over_blocks(shift[:, :]), ALU.mult))
            link(dve.tensor_reduce(brow[:, :], bcmp[:, :, :], AX.X, ALU.add))
            link(dve.scalar_tensor_tensor(out=brow[:, :], in0=t_blk[:, :, 0], scalar=float(P), in1=brow[:, :],
                                          op0=ALU.mult, op1=ALU.subtract))
            link(dve.tensor_scalar(btab[:, 1, :], brow[:, :], float(XR - P), None, ALU.min))
            dve.tensor_copy(btab[:, 0, :], bexp[:, :]).then_inc(btab_done, 1)
            link(dve.tensor_tensor(moved[:, :, :], sel[:, :, :, :].rearrange("p a t e -> p (a t) e"),
                                   shift[:, :].unsqueeze(1).to_broadcast([P, 2 * NT, E]), ALU.mult))
            link(dve.tensor_reduce(ypos[:, :, :].rearrange("p a t -> p (a t)"), moved[:, :, :], AX.X, ALU.add))
            link(dve.tensor_tensor(ypos[:, :, :], ypos[:, :, :], slot[:, :, :], ALU.add))
            link(dve.tensor_copy(ypos_i[:, :, :], ypos[:, :, :]))
            assert steps[0] == TABLE_OPS

            def ffn(k, j, r):
                if has(k, 2):
                    dve.wait_ge(x_hi, k + 3)
                    low_half(xT[:, j, 1, :, :], b_t[:, 0:D].rearrange("p (k s) -> p k s", k=KT), 1.0,
                             xT[:, j, 0, :, :]).then_inc(x_lo, 1)
                if has(k, 0):
                    dve.wait_ge(g_hi, k + 1)
                    low_half(gT[:, 1, :, :], b_pt[:, :].rearrange("p (k s) -> p k s", k=FT),
                             G_UP / (2 * W_UP * W_UP), gT[:, 0, :, :]).then_inc(g_lo, 1)
                if has(k, 1):
                    dve.wait_ge(tanhed, k + 2)
                    wait(dve, gg_done, k + 1)
                    dve.scalar_tensor_tensor(out=ua[:, :], in0=th[:, :], scalar=1.0, in1=b_a[(j + 1) % 2][:, :],
                                             op0=ALU.add, op1=ALU.mult).then_inc(u_done, 1)
                if has(k, 1):
                    dve.wait_ge(u_done, k + 2)
                    dve.wait_ge(b_mm, k + 2)
                    dve.tensor_tensor(gg[:, :], ua[:, :], b_s[:, :], ALU.mult).then_inc(gg_done, 1)

            all_blocks(ffn, dve)
            dve.wait_ge(gb_in, 16)
            with dve.Fori(0, NT // 4) as r:
                for k in range(4):
                    t = r * 4 + k
                    tile = bass.ds(t, 1)
                    dve.wait_ge(yg_in[k], r * 32 + 32)
                    dve.tensor_scalar(yg[:, k, 0, :], yg[:, k, 0, :], wts[:, 0, tile], None, ALU.mult) \
                        .then_inc(fin, 1)
                    dve.wait_ge(fin, r * 12 + (3 * k + 1))
                    dve.scalar_tensor_tensor(out=yg[:, k, 0, :], in0=yg[:, k, 1, :], scalar=wts[:, 1, tile],
                                             in1=yg[:, k, 0, :], op0=ALU.mult, op1=ALU.add).then_inc(fin, 1)
                    dve.wait_ge(fin, r * 12 + (3 * k + 2))
                    dve.tensor_tensor(yg[:, k, 0, :], yg[:, k, 0, :],
                                      gbB[:, bass.ds(r * 2 + k // 2, 1), :].squeeze(1), ALU.mult).then_inc(fin, 1)
                    dve.wait_ge(fin, r * 12 + (3 * k + 3))
                    dve.tensor_tensor(xs[:, tile, :].squeeze(1), xs[:, tile, :].squeeze(1), yg[:, k, 0, :],
                                      ALU.add).then_inc(fin_done, 1)

        @block.tensor
        def _(pe):
            pe.wait_ge(c_s, 2)
            pe.wait_ge(wmod_in, 16)
            for j in range(2 * KT):
                for kt in range(KT):
                    m = pe.matmul(b_qk[:, j * B:(j + 1) * B], wmod_sb[:, kt, j * P:(j + 1) * P],
                                  c_silu[:, kt, :], start=(kt == 0), stop=(kt == KT - 1))
            m.then_inc(mod_mm, 1)
            pe.wait_ge(consts, 7)

            def first(i):
                if i == -3:
                    for ps, kinds in ((b_ln, (2, 5)), (b_pv, (4, 3))):
                        for g, kind in enumerate(kinds):
                            for kt in range(KT):
                                m = pe.matmul(ps[0:B, g * D:(g + 1) * D], c_silu[:, kt, :],
                                              wmod_sb[:, kt, kind * D:(kind + 1) * D], start=(kt == 0),
                                              stop=(kt == KT - 1))
                    m.then_inc(g_mm, 1)
                if i == 0:
                    pe.wait_ge(small_in, 32)
                if i <= HQ:
                    pe.wait_ge(w_lo, min(NCH, -(-(i + HQ + 1) * 3 * KT * DH // CH)) if i < HQ else NCH)

            def prep(b, piece):
                if piece == "transpose":
                    pe.wait_ge(ln_z, b * TT + TT)
                    for kt in range(KT):
                        for t in range(TT):
                            m = pe.transpose(b_acc[:, kt * S + t * P:kt * S + (t + 1) * P],
                                             z[:, t, kt * P:(kt + 1) * P], ident[:, :])
                    m.then_inc(ln_t, 1)

            def product(out, stat, mov, n=KT):
                for q, (a, c_) in enumerate(PASSES):
                    for k in range(n):
                        m = pe.matmul(out, stat(a, k), mov(c_, k), start=(q == 0 and k == 0),
                                      stop=(q == len(PASSES) - 1 and k == n - 1))
                return m

            def tokens(b, t):
                return lambda a, k: hT[:, a, b, k, t * P:(t + 1) * P] if isinstance(b, int) else \
                    hT[:, a, bass.ds(b, 1), k, t * P:(t + 1) * P].squeeze(1)

            def weights(h, first, step, width):
                start = h * (3 * KT * DH) + first
                return lambda a, k: qkv16[:, a, bass.ds(start + k * step, width)]

            def step(i, j, b, h, g):
                if exists(i, 2):
                    pe.wait_ge(rope_done, i + 3)
                    wait(pe, t_lo, i + 2)
                    for a in range(2):
                        for t in range(TT):
                            m = pe.transpose(b_t[:, a * S + t * P:a * S + (t + 1) * P],
                                             rot[:, j % 2, (t * 2 + a) * DH:(t * 2 + a + 1) * DH], ident[:, :])
                    m.then_inc(t_mm, 1)
                if exists(i, 3):
                    bb, hh = at(i, b, h, 3)
                    wait(pe, v_lo, i + 3)
                    for t in range(TT):
                        m = product(b_v[:, t * DH:(t + 1) * DH], tokens(bb, t),
                                    weights(hh, 2 * KT * DH, DH, DH))
                    m.then_inc(v_mm, 1)
                if exists(i, 4):
                    bb, hh = at(i, b, h, 4)
                    if isinstance(hh, int) and hh == 0:
                        pe.wait_ge(ln_lo, bb + 1)
                    wait(pe, rot_done, i + 4)
                    for t in range(TT):
                        m = product(b_qk[:, t * 2 * DH:(t + 1) * 2 * DH], tokens(bb, t),
                                    weights(hh, 0, 2 * DH, 2 * DH))
                    m.then_inc(qk_mm, 1)

                if exists(i, 0):
                    pe.wait_ge(pt_lo, i + 1)
                    pe.wait_ge(v_lo, i + 1)
                    wait(pe, o_lo, i)
                    product(b_pv[:, 0:S], lambda a, k: v16[:, j % 4, a, k * DH:(k + 1) * DH],
                            lambda a, k: pT[:, a, k, :]).then_inc(pv_mm, 1)
                if exists(i, 2):
                    q2 = j % 2
                    pe.wait_ge(t_lo, i + 3)
                    wait(pe, exped, i + 2)
                    for t in range(TT):
                        m = product(b_s[:, t * S:(t + 1) * S],
                                    lambda a, k: qkT[:, q2, a, t * P:(t + 1) * P],
                                    lambda a, k: qkT[:, q2, a, S:2 * S], 1)
                    m.then_inc(s_mm, 1)
                if exists(i, 1):
                    pe.wait_ge(normed, i + 2)
                    wait(pe, pt_lo, i + 1)
                    for k in range(KT):
                        for t in range(TT):
                            m = pe.transpose(b_pt[:, k * S + t * P:k * S + (t + 1) * P],
                                             ex[:, (j + 1) % 2, t, k * P:(k + 1) * P], ident[:, :])
                    m.then_inc(pt_mm, 1)
            def late(b, piece):
                if piece == "project":
                    pe.wait_ge(o_lo, b * H + H)
                    for t in range(TT):
                        m = product(b_acc[:, t * D:(t + 1) * D],
                                    lambda a, k: oT[:, a, k, t * P:(t + 1) * P],
                                    lambda a, k: wo16[:, a, k, :], H)
                    m.then_inc(o_mm, 1)
                if piece == "transpose":
                    pe.wait_ge(h2_done, b * 2 + 2)
                    for kt in range(KT):
                        for t in range(TT):
                            m = pe.transpose(b_ln[:, kt * S + t * P:kt * S + (t + 1) * P],
                                             h2[:, t, kt * P:(kt + 1) * P], ident[:, :])
                    m.then_inc(h2_t, 1)
                if piece == "logits":
                    pe.wait_ge(h2_copy, b + 1)
                    for t in range(TT):
                        for kt in range(KT):
                            m = pe.matmul(b_ln[:, t * E:(t + 1) * E], h2T[:, kt, t * P:(t + 1) * P],
                                          gw_sb[:, kt * E:(kt + 1) * E], start=(kt == 0), stop=(kt == KT - 1))
                    m.then_inc(logit_mm, 1)
                if piece == "kept":
                    pe.wait_ge(rt, b * ROUTE_OPS + M16_AT)
                    for t in range(TT + 1):
                        for k in range(min(t + 1, TT)):
                            m = pe.matmul(b_ln[:, 32 + t * E:32 + (t + 1) * E],
                                          (tri16 if k == t else ones16)[:, :], m16[:, k, :],
                                          start=(k == 0), stop=(k == min(t, TT - 1)))
                    m.then_inc(rank_mm, 1)

            run_heads(step, late, prep, first, pe)
            pe.wait_ge(btab_done, 1)

            last = [None]

            def expert(k):
                return pe.value_load(btab[0:1, 0, bass.ds(k, 1)], min_val=0, max_val=E - 1)

            def ffn(k, j, r):
                if has(k, 2):
                    pe.wait_ge(xg_in[j], r * 16 + 32)
                    wait(pe, x_lo, k + 2)
                    for kt in range(KT):
                        m = pe.transpose(b_t[:, kt * P:(kt + 1) * P], xg[:, j, kt * P:(kt + 1) * P], ident[:, :])
                    m.then_inc(xt_mm, 1)
                if has(k, 0):
                    pe.wait_ge(gg_done, k + 1)
                    wait(pe, g_lo, k)
                    for q in range(FT):
                        m = pe.transpose(b_pt[:, q * P:(q + 1) * P], gg[:, q * P:(q + 1) * P], ident[:, :])
                    m.then_inc(gt_mm, 1)
                stat = lambda a, q: xT[:, (j + 1) % 2, a, q, :]
                if has(k, 1):
                    e1 = expert(k + 1)
                    col = e1 * (2 * FW)
                    pe.wait_ge(w_ffn, e1 * 16 + 16)
                    pe.wait_ge(x_lo, k + 2)
                    wait(pe, u_done, k)
                    product(b_a[(j + 1) % 2][:, :], stat,
                            lambda a, q: arena[:, bass.ds(col + (a * FW + q * F), F)]).then_inc(a_mm, 1)
                if has(k, 1):
                    product(b_s[:, :], stat,
                            lambda a, q: arena[:, bass.ds(col + (a * FW + KT * F + q * F), F)]) \
                        .then_inc(b_mm, 1)
                if has(k, 0):
                    col0 = (last[0] if j == 1 and last[0] is not None else expert(k)) * (2 * FW)
                    pe.wait_ge(g_lo, k + 1)
                    wait(pe, y_out, k)
                    product(b_pv[:, 0:D], lambda a, q: gT[:, a, q, :],
                            lambda a, q: arena[:, bass.ds(col0 + (a * FW + 2 * KT * F + q * D), D)], FT) \
                        .then_inc(y_mm, 1)
                last[0] = e1 if has(k, 1) else None

            all_blocks(ffn, pe)


def kernel(**inputs):
    import numpy as np
    import concourse.bacc as bacc
    from concourse.bass_utils import run_bass_kernel_spmd as run

    a = {k: np.asarray(v) for k, v in inputs.items()}
    x = a["L0_attn_x"].reshape(T, D)
    c = a["L0_c"].T.reshape(KT, P, B).transpose(1, 0, 2).reshape(P, KT * B)
    wmod = a["L0_wmod"].reshape(KT, P, NMOD * D).transpose(1, 0, 2)
    w = a["L0_attn_w_qkv"].reshape(3, H, DH, KT, P)
    qk = w[:2].transpose(4, 1, 3, 0, 2).reshape(P, H, KT * 2 * DH)
    v = w[2].transpose(3, 0, 2, 1).reshape(P, H, KT * DH)
    wo = a["L0_attn_w_out"].reshape(D, H, DH).transpose(2, 1, 0).reshape(P, H * D)
    wall = np.concatenate([np.concatenate([qk, v], axis=2).reshape(P, WCOLS), wo], axis=1)
    inv = (1.0 / np.float32(10000.0) ** (np.arange(0, DH, 2, dtype=np.float32) / np.float32(DH))).astype(np.float32)
    ang = np.arange(S, dtype=np.float32)[:, None] * inv[None, :]
    up = float(DH) ** -0.25 / W_UP
    cos, sin = np.cos(ang) * up, np.sin(ang) * up
    cos2 = np.concatenate([cos, cos], 1).reshape(TT, P, DH)
    sin2 = np.concatenate([-sin, sin], 1).reshape(TT, P, DH)
    rope = np.stack([np.repeat(t.transpose(1, 0, 2)[:, :, None], 2, axis=2).reshape(P, TT * 2 * DH)
                     for t in (cos2, sin2)], 1).astype(np.float32)
    gate_w = a["L0_ffn_gate_w"].reshape(E, KT, P).transpose(2, 1, 0).reshape(P, KT * E)
    w1, w3 = (a[k].reshape(E, F, KT, P).transpose(0, 3, 2, 1).reshape(E, P, KT * F)
              for k in ("L0_ffn_w1", "L0_ffn_w3"))
    w2 = a["L0_ffn_w2"].reshape(E, D, FT, P).transpose(0, 3, 2, 1).reshape(E, P, FT * D)
    fw = np.concatenate([w1, w3, w2], axis=2)
    e, blk = np.arange(E), np.arange(NB)
    table = np.concatenate([np.tile(E - e, TT), e * T, np.tile(P * np.arange(NT), E),
                            np.repeat(blk, E), np.tile(e, NB)]).astype(np.float32)
    table = np.tile(table, (P, 1))
    assert table.shape == (P, TABLE)
    data = {"in_x": x, "in_c": c, "in_wmod": wmod, "in_rope": rope, "in_wall": wall,
            "in_gate_w": gate_w, "in_fw": fw, "in_table": table}
    data = {k: np.ascontiguousarray(t) for k, t in data.items()}
    nc = bacc.Bacc("TRN2", target_bir_lowering=False, num_devices=1)
    aps = [nc.dram_tensor(k, t.shape, F32, kind="ExternalInput").ap() for k, t in data.items()]
    out = nc.dram_tensor("out_x", (B, S, D), F32, kind="ExternalOutput").ap()
    scratch = [nc.dram_tensor(k, shape, dt, kind="Internal").ap() for k, shape, dt in (
        ("mod_rows", (B, 4 * D), F32), ("ffn_halves", (E, P, 2, FW), F16),
        ("expert_rows", (XR, D), F32), ("result_rows", (NB * P, D), F32))]
    build(nc, *aps, out, *scratch)
    r = run(nc, [data], core_ids=[0])
    return r.results[0]["out_x"]
```

```python
from contextlib import ExitStack

import concourse.bass as bass
from concourse import mybir

F32 = mybir.dt.float32
F16 = mybir.dt.float16
I32 = mybir.dt.int32
ALU = mybir.AluOpType
ACT = mybir.ActivationFunctionType
AX = mybir.AxisListType

P = 128
B, S, D = 8, 256, 256
H, DH = 16, 128
E, F = 8, 512
T = B * S
NT = T // P
TT = S // P
KT = D // P
NMOD = 6
EPS = 1e-5
GATE_FLOOR = 0.25

W_UP = 64.0
V_UP = 16.0
P_UP = 256.0
O_UP = 16.0
PASSES = ((0, 0), (0, 1), (1, 0))

HQ = 4
NG = H // HQ
FT = F // P
FW = 2 * KT * F + FT * D
FPART = FW // NG
NB = 2 * T // P + E - 1
EARLY = 14
assert ((B - 2) * S * 2 - E * (P - 1)) // P >= EARLY
XS = T + P
XW = D + 2
G_UP = 16.0
FAR = 3.0e38
JITTER = 0.02

LATE = ["gate", "add", "statistics", "moments", "normalise", "shift", "transpose", "logits",
        "first", "second", "both", "kept", "weights", "rows", "scatter 0", "scatter 1"]
PREP = ["normalise", "transpose", "modulate", "low half"]
BETWEEN = {-2: ["project", "gate", "add"], -1: ["statistics", "moments"], 0: ["normalise"], 1: ["shift"],
           2: ["transpose"], 3: ["logits", "first"], 4: ["second"], 5: ["both"], 6: ["kept", "weights"],
           7: ["rows", "scatter 0", "count", "tails 0"], 8: ["scatter 1", "sum", "tails 1"],
           9: ["shifts", "experts"], 10: ["first rows"]}
assert [p for k in BETWEEN for p in BETWEEN[k] if p in LATE] == LATE
EARLY_TABLE = {5: "count", 6: "sum", 7: "shifts", 8: "experts", 14: "first rows"}

CHAIN = {"first": 0, "second": 7, "both": 12, "kept": 15, "weights": 17, "rows": 22}
M16_AT, EXP_AT, ROUTE_OPS = 13, 14, 26
TABLE_AT = {"count": (0, 0), "sum": (4, 5), "shifts": (10, 11), "experts": (14, 14), "first rows": (17, 17)}
TABLE_OPS = 23

TABLE = 24 + E * NT + 2 * NB * E + NT + NB
YR = 2 * (T + 1)
WCOLS = H * 3 * KT * DH
WALL = WCOLS + H * D
NCH = 16
CH = WALL // NCH
ORDER = (0, 1, 2, 3, 12, 4, 5, 6, 7, 13, 8, 9, 10, 14, 11, 15)
STAGES = 3
assert len(ORDER) == NCH and WALL - WCOLS == 4 * CH and WCOLS == 12 * CH


def chunks_before(i):
    if i == -HQ:
        return range(1, STAGES)
    n = STAGES + (i + HQ - 1)
    return range(n, n + 1) if n < NCH else ()


def chunks_for(i):
    heads = min(i + 5, H)
    used = set(range(-(-heads * 3 * KT * DH // CH)))
    if i > 0:
        used |= {12 + n for n in range((i - 1) // (CH // D) + 1)}
    return 1 + max(ORDER.index(n) for n in used)


def build(nc, x, c, wmod, rope, wall, gate_w, fw, table, out, mscr, wscr, xrows, yrows):
    with ExitStack() as ctx:
        def sb(name, shape, dt=F32):
            return ctx.enter_context(nc.sbuf_tensor(name, shape, dt))

        def bank(name):
            return ctx.enter_context(nc.psum_tensor(name, [P, 512], F32))

        def sem(name):
            return ctx.enter_context(nc.semaphore(name))

        arena = sb("arena", [P, E * 2 * FW], F16)
        spans = (2 * WCOLS, 2 * B * KT * S, 2 * H * D, 2 * H * S)
        assert sum(spans) == E * 2 * FW
        cuts = [sum(spans[:i]) for i in range(5)]
        qkv16 = arena[:, cuts[0]:cuts[1]].rearrange("p (a n) -> p a n", a=2)
        hT = arena[:, cuts[1]:cuts[2]].rearrange("p (a b k s) -> p a b k s", a=2, b=B, k=KT)
        wo16 = arena[:, cuts[2]:cuts[3]].rearrange("p (a h n) -> p a h n", a=2, h=H)
        oT = arena[:, cuts[3]:cuts[4]].rearrange("p (a h s) -> p a h s", a=2, h=H)
        wmod_sb = arena[:, cuts[3]:cuts[3] + 2 * KT * NMOD * D].bitcast(F32) \
            .rearrange("p (k n) -> p k n", k=KT)
        xs = sb("xs", [P, NT, D])
        stage = sb("stage", [P, 1 + STAGES, CH])
        split16 = sb("split16", [P, 2, FPART], F16)
        rope_sb = sb("rope_sb", [P, 2, TT * 2 * DH])
        c_sb = sb("c_sb", [P, KT * B])
        c_tanh = sb("c_tanh", [P, KT * B])
        c_silu = sb("c_silu", [P, KT, B])
        modT = sb("modT", [P, 2 * KT, B])
        g_sign = sb("g_sign", [B, 2 * D])
        g_abs = sb("g_abs", [B, 2 * D])
        m_row = sb("m_row", [B, 4, D])
        mB = sb("mB", [P, 4, D])
        held = sb("held", [P, 2])
        zeros = sb("zeros", [P, XW])
        stats = sb("stats", [P, NT, 6])
        mv = sb("mv", [P, NT, 2])
        rstd = sb("rstd", [P, NT])
        half_neg = sb("half_neg", [P, NT])
        z = sb("z", [P, TT, D])
        hmod = sb("hmod", [P, KT, S])
        h2 = sb("h2", [P, TT, XW])
        h2T = sb("h2T", [P, KT, S])
        gw_sb = sb("gw_sb", [P, KT * E])
        ident = sb("ident", [P, P])
        qkc = sb("qkc", [P, 2, 512])
        rot = sb("rot", [P, 2, 512])
        qkT = sb("qkT", [P, 2, 2, 512], F16)
        v16 = sb("v16", [P, 4, 2, TT * DH], F16)
        ex = sb("ex", [P, 2, TT, S])
        pT = sb("pT", [P, 2, KT, S], F16)
        nmax = sb("nmax", [P, 2, TT])
        esum = sb("esum", [P, 2, TT])
        rsum = sb("rsum", [P, 2, TT])
        gated = sb("gated", [P, TT, D])
        table_sb = sb("table_sb", [P, TABLE])
        tri16 = sb("tri16", [P, P], F16)
        ones16 = sb("ones16", [P, P], F16)
        lg = sb("lg", [P, 2, TT, E])
        hit = sb("hit", [P, TT, E])
        second = sb("second", [P, TT])
        top = sb("top", [P, 2, TT])
        sel = sb("sel", [P, 2, TT, E])
        absl = sb("absl", [P, 2, TT, E])
        diff = sb("diff", [P, 2, TT, E])
        keep = sb("keep", [P, 2, TT, E])
        ediff = sb("ediff", [P, 2, TT, E])
        psum_ = sb("psum_", [P, 2, TT])
        wts = sb("wts", [P, 2, NT])
        m16 = sb("m16", [P, TT, E], F16)
        base = sb("base", [P, E])
        row = sb("row", [P, TT, E])
        srow = sb("srow", [P, 2, TT, E])
        slot = sb("slot", [P, 2, TT])
        slot_i = sb("slot_i", [P, 2, TT], I32)
        cnt = sb("cnt", [P, E])
        gone = sb("gone", [P, E])
        over = sb("over", [P, E, NT])
        ends = sb("ends", [P, 2, E])
        shift = sb("shift", [P, E])
        free_i = sb("free_i", [P, E], I32)
        bcmp = sb("bcmp", [P, NB, E])
        bexp = sb("bexp", [P, NB])
        brow = sb("brow", [P, NB])
        bfirst = sb("bfirst", [P, NB])
        code = sb("code", [P, NB])
        spare = sb("spare", [P, 2])
        code_i = sb("code_i", [P, 2], I32)
        btab = sb("btab", [P, 2, NB], I32)
        xg = sb("xg", [P, 2, XW])
        xT = sb("xT", [P, 2, 2, KT, P], F16)
        th = sb("th", [P, F])
        ua = sb("ua", [P, F])
        gg = sb("gg", [P, F])
        gT = sb("gT", [P, 2, FT, P], F16)
        y_sb = sb("y_sb", [P, 2, D])
        yg = arena[:, 0:B * 4 * TT * D].bitcast(F32).rearrange("p (b q t n) -> p b q t n", b=B, q=2, t=TT)
        gbB = stage[:, 2:4, :].rearrange("p a (j n) -> p (a j) n", n=D)

        t_first = table_sb[:, 0:TT * E].rearrange("p (t e) -> p t e", e=E)
        t_base = table_sb[:, 16:24]
        t_thr = table_sb[:, 24:24 + E * NT].rearrange("p (e k) -> p e k", k=NT)
        o = 24 + E * NT
        t_blk = table_sb[:, o:o + NB * E].rearrange("p (k e) -> p k e", e=E)
        t_exp = table_sb[:, o + NB * E:o + 2 * NB * E].rearrange("p (k e) -> p k e", e=E)
        t_token = table_sb[:, o + 2 * NB * E:TABLE - NB]
        t_spare = table_sb[:, TABLE - NB:TABLE]

        b_qk, b_v, b_t, b_pt, b_s, b_pv, b_acc, b_ln = (
            bank(n) for n in ("b_qk", "b_v", "b_t", "b_pt", "b_s", "b_pv", "b_acc", "b_ln"))

        b_a = (b_qk, b_v)

        x_in, x_rest_in, small_in = sem("x_in"), sem("x_rest_in"), sem("small_in")
        w_in = [sem(f"w_in{i}") for i in range(STAGES)]
        w_hi, w_lo = sem("w_hi"), sem("w_lo")
        consts = sem("consts")
        c_t, c_s = sem("c_t"), sem("c_s")
        c_in, wmod_in, wmod_rest_in, rope_in, mod_done = (
            sem(n) for n in ("c_in", "wmod_in", "wmod_rest_in", "rope_in", "mod_done"))
        mod_mm, mod_sb, g_mm, g_done, g_out, m_in = (
            sem(n) for n in ("mod_mm", "mod_sb", "g_mm", "g_done", "g_out", "m_in"))
        ln_stat, ln_mv, ln_rstd, ln_z, ln_t, ln_hi, ln_mod, ln_lo = (
            sem(n) for n in ("ln_stat", "ln_mv", "ln_rstd", "ln_z", "ln_t", "ln_hi", "ln_mod", "ln_lo"))
        qk_mm, v_mm, t_mm, s_mm, pt_mm, pv_mm, o_mm = (
            sem(n) for n in ("qk_mm", "v_mm", "t_mm", "s_mm", "pt_mm", "pv_mm", "o_mm"))
        qk_copied, v_hi, t_hi, exped, pt_hi, o_hi = (
            sem(n) for n in ("qk_copied", "v_hi", "t_hi", "exped", "pt_hi", "o_hi"))
        rot_done, v_lo, t_lo, maxed, rsummed, pt_lo, o_lo, gate_done, x1_done = (
            sem(n) for n in ("rot_done", "v_lo", "t_lo", "maxed", "rsummed", "pt_lo", "o_lo",
                             "gate_done", "x1_done"))
        cos_done, rope_done, normed = sem("cos_done"), sem("rope_done"), sem("normed")
        fw_in, fw_hi, fw_lo, fw_out, w_ffn = (sem(n) for n in ("fw_in", "fw_hi", "fw_lo", "fw_out", "w_ffn"))
        l2_stat, l2_mv, l2_rstd, l2_z, h2_done, h2_t, h2_copy, logit_mm, rt, rt_exp, rank_mm = (
            sem(n) for n in ("l2_stat", "l2_mv", "l2_rstd", "l2_z", "h2_done", "h2_t", "h2_copy",
                             "logit_mm", "rt", "rt_exp", "rank_mm"))
        scattered, bt, btab_done = sem("scattered"), sem("bt"), sem("btab_done")
        xg_in = [sem(f"xg_in{i}") for i in range(2)]
        y_st = [sem(f"y_st{i}") for i in range(2)]
        xt_mm, a_mm, gt_mm, b_mm, y_mm = (sem(n) for n in ("xt_mm", "a_mm", "gt_mm", "b_mm", "y_mm"))
        x_hi, tanhed, g_hi, y_out = (sem(n) for n in ("x_hi", "tanhed", "g_hi", "y_out"))
        x_lo, u_done, g_lo, gg_done = (sem(n) for n in ("x_lo", "u_done", "g_lo", "gg_done"))
        tails, tails_zero, tails_zero_too, coding, coded, code_out, held_done = (
            sem(n) for n in ("tails", "tails_zero", "tails_zero_too", "coding", "coded", "code_out", "held_done"))
        yg_in = [sem(f"yg_in{i}") for i in range(B)]
        gb_in, stored = sem("gb_in"), sem("stored")
        fin_first, fin_both, fin_gated, fin_done = (
            sem(n) for n in ("fin_first", "fin_both", "fin_gated", "fin_done"))

        block = ctx.enter_context(nc.Block())

        def batch_steps(n, step, late, prep, first=None):
            for g in range(NG):
                for j in range(HQ):
                    if first:
                        first(g * HQ + j)
                    step(n * H + (g * HQ + j), j, n, g * HQ + j, g)
                    if late:
                        late(n - 1, LATE[g * HQ + j])
                    if prep and g * HQ + j < len(PREP):
                        prep(n + 1, PREP[g * HQ + j])

        def run_heads(step, late, prep, first, eng):
            for piece in PREP:
                prep(0, piece)
            for i in range(-HQ, 0):
                first(i)
                step(i, i % HQ, 0, i, 0)
            batch_steps(0, step, None, prep, first)
            with eng.Fori(1, B - 1) as n:
                batch_steps(n, step, late, prep)
            batch_steps(B - 1, step, late, None)

        def head_out(half, h):
            return oT[:, half, h, :]

        def weights_chunk(half, n):
            if n * CH < WCOLS:
                return qkv16[:, half, n * CH:(n + 1) * CH]
            first = (n * CH - WCOLS) // D
            return wo16[:, half, first:first + CH // D, :].rearrange("p h n -> p (h n)")

        def exists(i, ahead):
            return not isinstance(i, int) or 0 <= i + ahead < B * H

        def at(i, b, h, ahead):
            if isinstance(i, int):
                return divmod(i + ahead, H)
            if h + ahead < H:
                return b, h + ahead
            return b + 1, h + ahead - H

        def wait(eng, s, value):
            if not (isinstance(value, int) and value <= 0):
                eng.wait_ge(s, value)

        def all_blocks(step, late, eng):
            for k in range(-2, 12):
                step(k, k % 2, (k - k % 2) // 2, k % 4)
                for piece in BETWEEN.get(k, ()):
                    late(B - 1, piece)
            with eng.Fori(3, (NB - 4) // 4) as r:
                for j in range(4):
                    step(r * 4 + j, j % 2, r * 2 + j // 2, j)
            for k in range((NB - 4) // 4 * 4, NB):
                step(k, k % 2, k // 2, k % 4)

        def has(k, ahead):
            return not isinstance(k, int) or 0 <= k + ahead < NB

        def zero_tails(eng, first):
            eng.wait_ge(tails, 1)
            for e in (first, first + 1):
                row = eng.value_load(free_i[0:1, e:e + 1], min_val=e * XS, max_val=e * XS + T)
                eng.dma_start(xrows[bass.ds(row, P), :], zeros[:, :]) \
                    .then_inc(tails_zero if e < E // 2 else tails_zero_too, 16)

        @block.sync
        def _(sp):
            xt = x.rearrange("(t p) n -> p t n", p=P)
            sp.dma_start(xs[:, 0:TT, :], xt[:, 0:TT, :]).then_inc(x_in, 16)

            def chunk_in(n):
                if n >= STAGES:
                    sp.wait_ge(w_lo, n + 1 - STAGES)
                sp.dma_start(stage[:, 1 + n % STAGES, :], wall[:, ORDER[n] * CH:(ORDER[n] + 1) * CH]) \
                    .then_inc(w_in[n % STAGES], 16)

            for n in range(STAGES):
                chunk_in(n)
            sp.dma_start(xs[:, TT:NT, :], xt[:, TT:NT, :]).then_inc(x_rest_in, 16)
            chunk_in(STAGES)
            chunk_in(STAGES + 1)
            sp.dma_start(stage[:, 0, 0:FPART], fw[0, :, 0:FPART]).then_inc(fw_in, 16)
            for n in range(STAGES + 2, 13):
                chunk_in(n)
                if n == 9:
                    sp.wait_ge(g_done, 3)
                    sp.dma_start(mscr, m_row[:, :, :].rearrange("b k n -> b (k n)")).then_inc(g_out, 16)
            sp.wait_ge(g_out, 16)
            sp.dma_start(mB[:, :, :], mscr[0:1, :].partition_broadcast(P)).then_inc(m_in, 16)

            def part_out(b, g):
                sp.wait_ge(fw_lo, b * NG + (g + 1))
                dst = wscr[b, :, :, g * FPART:(g + 1) * FPART] if isinstance(b, int) else \
                    wscr[bass.ds(b, 1), :, :, g * FPART:(g + 1) * FPART].squeeze(0)
                sp.dma_start(dst, split16[:, :, :]).then_inc(fw_out, 16)

            def part_in(b, g):
                src = fw[b, :, g * FPART:(g + 1) * FPART] if isinstance(b, int) else \
                    fw[bass.ds(b, 1), :, g * FPART:(g + 1) * FPART].squeeze(0)
                sp.dma_start(stage[:, 0, 0:FPART], src).then_inc(fw_in, 16)

            def next_part(b, g):
                part_out(b, g)
                if isinstance(g, int) and g + 1 < NG:
                    part_in(b, g + 1)
                elif not isinstance(b, int):
                    part_in(b + 1, 0)

            next_part(0, 0)
            for n in range(13, NCH):
                chunk_in(n)
            next_part(0, 1)
            with sp.Fori(1, B) as b:
                next_part(b - 1, 2)
                next_part(b - 1, 3)
                next_part(b, 0)
                next_part(b, 1)
                sp.wait_ge(h2_done, b * 2)
                sp.dma_start(mB[:, :, :], mscr[bass.ds(b, 1), :].partition_broadcast(P)).then_inc(m_in, 16)
            next_part(B - 1, 2)
            sp.wait_ge(fw_out, 16 * (B * NG - 1))
            sp.wait_ge(v_mm, B * H)
            sp.wait_ge(qk_mm, B * H)
            for e in range(E):
                if e == 1:
                    next_part(B - 1, 3)
                if e == E - 1:
                    sp.wait_ge(fw_out, 16 * B * NG)
                if e * 2 * FW + 2 * FW > cuts[2]:
                    sp.wait_ge(o_mm, B)
                for a in range(2):
                    sp.dma_start(arena[:, (e * 2 + a) * FW:(e * 2 + a + 1) * FW],
                                 wscr[e, :, a, :]).then_inc(w_ffn, 16)
                    sp.wait_ge(w_ffn, 16 * (e * 2 + a + 1))
            sp.dma_start(gbB, mscr[:, D:2 * D].unsqueeze(0).partition_broadcast(P)).then_inc(gb_in, 16)
            for j in range(2):
                sp.wait_ge(y_st[j], 16 * ((NB + 1 - j) // 2))
            results = yrows[0:YR].rearrange("(q r) n -> r q n", q=2)

            def fetch(b):
                for t in range(TT):
                    row = 1 + b * S + t * P
                    sp.dma_start(yg[:, b, :, t, :], results[row:row + P]).then_inc(yg_in[b], 16)

            for b in range(B):
                fetch(b)
            for b in range(B):
                sp.wait_ge(fin_done, b + 1)
                sp.dma_start(out[b].rearrange("(t p) n -> p t n", p=P), xs[:, b * TT:(b + 1) * TT, :]) \
                    .then_inc(stored, 16)
            sp.wait_ge(stored, 16 * B)

        @block.gpsimd
        def _(pool):
            pool.memset(ident[:, :], 0.0).then_inc(consts, 1)
            pool.memset(tri16[:, :], 1.0).then_inc(consts, 1)
            pool.memset(half_neg[:, :], -0.5).then_inc(consts, 1)
            pool.memset(zeros[:, :], 0.0).then_inc(consts, 1)
            pool.memset(ones16[:, :], 1.0).then_inc(consts, 1)
            pool.dma_start(table_sb[:, :], table).then_inc(scattered, 16)
            pool.wait_ge(consts, 5)
            pool.affine_select(out=ident[:, :], in_=ident[:, :], compare_op=ALU.not_equal, fill=1.0,
                               base=0, pattern=[[-1, P]], channel_multiplier=1).then_inc(consts, 1)
            pool.affine_select(out=tri16[:, :], in_=tri16[:, :], compare_op=ALU.is_gt, fill=0.0,
                               base=0, pattern=[[1, P]], channel_multiplier=-1).then_inc(consts, 1)
            pool.wait_ge(ln_mv, TT + 1)
            pool.tensor_tensor(rstd[:, 0:TT], mv[:, 0:TT, 1], half_neg[:, 0:TT], ALU.pow).then_inc(ln_rstd, 1)
            pool.wait_ge(rope_in, 16)

            def first(i):
                for step_, a, b in ((0, TT, 2 * TT), (H - 1, 2 * TT, NT)):
                    if i == step_:
                        pool.wait_ge(ln_mv, b // TT * (TT + 1))
                        pool.tensor_tensor(rstd[:, a:b], mv[:, a:b, 1], half_neg[:, a:b], ALU.pow) \
                            .then_inc(ln_rstd, 1)

            def prep(b, piece):
                if piece == "low half":
                    pool.wait_ge(ln_mod, b * KT + KT)
                    pool.tensor_tensor(hT[:, 1, bass.ds(b, 1), :, :].squeeze(1), hmod[:, :, :],
                                       hT[:, 0, bass.ds(b, 1), :, :].squeeze(1), ALU.subtract) \
                        .then_inc(ln_lo, 1)

            def step(i, j, b, h, g):
                if exists(i, 4):
                    k = j % 2
                    pool.wait_ge(qk_copied, i + 5)
                    pool.tensor_tensor(qkc[:, k, :], qkc[:, k, :], rope_sb[:, 0, :], ALU.mult) \
                        .then_inc(cos_done, 1)
                    pool.wait_ge(cos_done, i + 5)
                    pool.wait_ge(rot_done, i + 5)
                    pool.tensor_tensor(rot[:, k, :], qkc[:, k, :], rot[:, k, :], ALU.add) \
                        .then_inc(rope_done, 1)
                if exists(i, 2):
                    e = ex[:, (j + 2) % 2, :, :]
                    pool.wait_ge(rsummed, i + 3)
                    pool.tensor_tensor(e, e, rsum[:, (j + 2) % 2, :].unsqueeze(2).to_broadcast([P, TT, S]),
                                       ALU.mult).then_inc(normed, 1)

            def late(b, piece):
                if piece == "moments":
                    pool.wait_ge(l2_mv, (b + 1) * (TT + 1))
                    pool.tensor_tensor(rstd[:, 0:TT], mv[:, 0:TT, 1], half_neg[:, 0:TT], ALU.pow) \
                        .then_inc(l2_rstd, 1)
                if piece == "normalise":
                    pool.wait_ge(scattered, b * 64 + 16)
                    pool.wait_ge(l2_z, (b + 1) * TT)
                    pool.wait_ge(m_in, (b + 1) * 16)
                    pool.tensor_tensor(h2[:, :, 0:D], z[:, :, :], mB[:, 2:3, :].to_broadcast([P, TT, D]),
                                       ALU.mult).then_inc(h2_done, 1)
                if piece == "shift":
                    pool.wait_ge(h2_done, b * 2 + 1)
                    pool.tensor_tensor(h2[:, :, 0:D], h2[:, :, 0:D], mB[:, 3:4, :].to_broadcast([P, TT, D]),
                                       ALU.add).then_inc(h2_done, 1)
                if piece in ("tails 0", "tails 1"):
                    zero_tails(pool, 4 + 2 * int(piece[-1]))
                if piece == "scatter 0":
                    pool.wait_ge(rt, (b + 1) * ROUTE_OPS)
                    pool.tensor_tensor(held[:, 0:1], half_neg[:, 0:1], half_neg[:, 1:2], ALU.mult)
                if piece in ("scatter 0", "scatter 1"):
                    q = int(piece[-1])
                    for t in range(TT):
                        pool.indirect_dma_start(
                            xrows, bass.IndirectOffsetOnAxis(ap=slot_i[:, q, t:t + 1], axis=0),
                            h2[:, t, :], None).then_inc(scattered, 16)

            run_heads(step, late, prep, first, pool)

            def put(k, j, r, part):
                if has(k, 0):
                    wait(pool, held_done, k)
                    pool.wait_ge(y_out, k + 1)
                    pool.wait_ge(code_out, k + 1)
                    pool.tensor_tensor(held[:, 1:2], half_neg[:, 0:1], half_neg[:, 1:2], ALU.mult) \
                        .then_inc(held_done, 1)
                    pool.indirect_dma_start(
                        yrows, bass.IndirectOffsetOnAxis(ap=code_i[:, j:j + 1], axis=0),
                        y_sb[:, j, :], None).then_inc(y_st[j], 16)

            all_blocks(put, late, pool)
            for b in range(B):
                y = yg[:, b, 1, :, :]
                pool.wait_ge(gb_in, 16)
                pool.wait_ge(fin_both, (b + 1) * TT)
                pool.tensor_tensor(y, y, gbB[:, b:b + 1, :].to_broadcast([P, TT, D]), ALU.mult) \
                    .then_inc(fin_gated, 1)

        @block.scalar
        def _(act):
            act.dma_start(c_sb[:, :], c).then_inc(c_in, 16)
            act.dma_start(wmod_sb[:, :, 0:2 * D], wmod[:, :, 0:2 * D]).then_inc(wmod_in, 16)
            act.dma_start(rope_sb[:, :, :], rope).then_inc(rope_in, 16)
            act.dma_start(wmod_sb[:, :, 2 * D:], wmod[:, :, 2 * D:]).then_inc(wmod_rest_in, 16)
            act.dma_start(gw_sb[:, :], gate_w).then_inc(small_in, 16)
            act.wait_ge(c_in, 16)
            act.activation(c_tanh[:, :], c_sb[:, :], ACT.Tanh, scale=0.5).then_inc(c_t, 1)

            def first(i):
                if i == -HQ:
                    chunks(chunks_before(i))

            def chunks(places):
                for n in places:
                    act.wait_ge(w_in[n % STAGES], n // STAGES * 16 + 16)
                    act.activation(weights_chunk(0, ORDER[n]), stage[:, 1 + n % STAGES, :], ACT.Copy, scale=W_UP) \
                        .then_inc(w_hi, 1)

            chunks([0])

            def prep(b, piece):
                if piece == "transpose":
                    act.wait_ge(mod_done, 2)
                    act.wait_ge(ln_t, b + 1)
                    for kt in range(KT):
                        act.activation(hT[:, 0, bass.ds(b, 1), kt, :].squeeze(1), b_ln[:, kt * S:(kt + 1) * S],
                                       ACT.Identity, bias=modT[:, kt, bass.ds(b, 1)],
                                       scale=modT[:, KT + kt, bass.ds(b, 1)]).then_inc(ln_hi, 1)

            def part_high(part):
                act.wait_ge(fw_in, part * 16 + 16)
                wait(act, fw_out, part * 16)
                act.activation(split16[:, 0, :], stage[:, 0, 0:FPART], ACT.Copy, scale=W_UP) \
                    .then_inc(fw_hi, 1)

            def step(i, j, b, h, g):
                if exists(i, 2):
                    act.wait_ge(t_mm, i + 3)
                    wait(act, s_mm, i + 1)
                    act.activation(qkT[:, j % 2, 0, :], b_t[:, :], ACT.Copy).then_inc(t_hi, 1)
                if exists(i, 3):
                    act.wait_ge(v_mm, i + 4)
                    wait(act, pv_mm, i)
                    act.activation(v16[:, (j + 3) % 4, 0, :], b_v[:, 0:TT * DH], ACT.Copy,
                                   scale=V_UP / W_UP).then_inc(v_hi, 1)
                if exists(i, 4):
                    act.wait_ge(qk_mm, i + 5)
                    wait(act, rope_done, i + 3)
                    act.activation(qkc[:, j % 2, :], b_qk[:, :], ACT.Copy).then_inc(qk_copied, 1)
                if exists(i, 0):
                    act.wait_ge(pv_mm, i + 1)
                    act.activation(head_out(0, h), b_pv[:, 0:S], ACT.Copy,
                                   scale=O_UP / (P_UP * V_UP)).then_inc(o_hi, 1)
                if isinstance(i, int) and i < H:
                    chunks(chunks_before(i + 1))
                if j == HQ - 1 and exists(i, 0):
                    part_high(b * NG + g)
                if exists(i, 1):
                    act.wait_ge(pt_mm, i + 2)
                    wait(act, pv_mm, i + 1)
                    act.activation(pT[:, 0, :, :], b_pt[:, :].rearrange("p (k s) -> p k s", k=KT),
                                   ACT.Copy, scale=P_UP).then_inc(pt_hi, 1)
                if exists(i, 2):
                    k = j % 2
                    act.wait_ge(maxed, i + 3)
                    wait(act, pt_mm, i + 1)
                    wait(act, rsummed, i + 1)
                    for t in range(TT):
                        e = act.activation(ex[:, k, t, :], b_s[:, t * S:(t + 1) * S], ACT.Exp,
                                           bias=nmax[:, k, t:t + 1], accum_out=esum[:, k, t:t + 1])
                    e.then_inc(exped, 1)
            def get(k, slot):
                start = act.value_load(btab[0:1, 1, bass.ds(k, 1)], min_val=0, max_val=E * XS - P)
                act.dma_start(xg[:, slot, :], xrows[bass.ds(start, P), :]).then_inc(xg_in[slot], 16)

            def late(b, piece):
                if piece == LATE[max(EARLY_TABLE)] and isinstance(b, int) and b == B - 2:
                    act.wait_ge(btab_done, 1)
                    act.wait_ge(scattered, (B - 2) * 64 + 16)
                    get(0, 0)
                    get(1, 1)
                if piece == "transpose":
                    act.wait_ge(h2_t, b + 1)
                    act.activation(h2T[:, :, :], b_ln[:, :].rearrange("p (k s) -> p k s", k=KT), ACT.Copy) \
                        .then_inc(h2_copy, 1)
                if piece in ("tails 0", "tails 1"):
                    zero_tails(act, 2 * int(piece[-1]))
                if piece == "kept":
                    act.wait_ge(rt, b * ROUTE_OPS + EXP_AT)
                    act.activation(ediff[:, :, :, :], diff[:, :, :, :], ACT.Exp).then_inc(rt_exp, 1)

            run_heads(step, late, prep, first, act)
            def ffn(k, j, r, part):
                if has(k, 2):
                    act.wait_ge(xt_mm, k + 3)
                    wait(act, b_mm, k + 1)
                    act.activation(xT[:, j, 0, :, :], b_t[:, 0:D].rearrange("p (k s) -> p k s", k=KT),
                                   ACT.Copy).then_inc(x_hi, 1)
                if has(k, 0):
                    act.wait_ge(gt_mm, k + 1)
                    wait(act, y_mm, k)
                    act.activation(gT[:, 0, :, :], b_pt[:, :].rearrange("p (k s) -> p k s", k=FT), ACT.Copy,
                                   scale=G_UP / (2 * W_UP * W_UP)).then_inc(g_hi, 1)
                if has(k, 1):
                    act.wait_ge(a_mm, k + 2)
                    wait(act, u_done, k + 1)
                    act.activation(th[:, :], b_a[(j + 1) % 2][:, :], ACT.Tanh, scale=0.5 / W_UP) \
                        .then_inc(tanhed, 1)
                if has(k, 4) and not (isinstance(k, int) and EARLY - 4 <= k < EARLY - 2):
                    act.wait_ge(coded, k + 3)
                    get(k + 4, j)
                if isinstance(k, int) and k == EARLY - 3:
                    act.wait_ge(coded, EARLY)
                    act.wait_ge(btab_done, 2)
                    act.wait_ge(scattered, B * 64 + 16)
                    act.wait_ge(tails_zero, 16 * (E // 2))
                    act.wait_ge(tails_zero_too, 16 * (E - E // 2))
                    get(EARLY, 0)
                    get(EARLY + 1, 1)
                if has(k, 0):
                    act.wait_ge(y_mm, k + 1)
                    wait(act, y_st[j], r * 16)
                    act.activation(y_sb[:, j, :], b_pv[:, 0:D], ACT.Copy).then_inc(y_out, 1)

            all_blocks(ffn, late, act)
            for t in range(NT):
                y = yg[:, t // TT, 0, t % TT, :]
                act.wait_ge(yg_in[t // TT], TT * 16)
                act.activation(y, y, ACT.Copy, scale=wts[:, 0, t:t + 1]).then_inc(fin_first, 1)

        @block.vector
        def _(dve):
            def low_half(out, full, scale, hi):
                return dve.scalar_tensor_tensor(out=out, in0=full, scalar=scale, in1=hi,
                                                op0=ALU.mult, op1=ALU.subtract)

            def statistics(a, b):
                before = dve_stats[0]
                for t in range(a, b):
                    dve.bn_stats(stats[:, t, :], xs[:, t, :]).then_inc(ln_stat, 1)
                dve.wait_ge(ln_stat, b)
                for t in range(a, b):
                    dve.bn_aggr(mv[:, t, :], stats[:, t, :]).then_inc(ln_mv, 1)
                dve.wait_ge(ln_mv, before + b - a)
                dve.tensor_scalar(mv[:, a:b, 1], mv[:, a:b, 1], EPS, None, ALU.add).then_inc(ln_mv, 1)
                dve_stats[0] += b - a + 1

            dve_stats = [0]
            dve.wait_ge(x_in, 16)
            statistics(0, TT)
            dve.wait_ge(c_t, 1)
            dve.wait_ge(c_in, 16)
            dve.scalar_tensor_tensor(out=c_tanh[:, :], in0=c_tanh[:, :], scalar=1.0, in1=c_sb[:, :],
                                     op0=ALU.add, op1=ALU.mult).then_inc(c_s, 1)
            dve.wait_ge(c_s, 1)
            dve.tensor_scalar(c_silu[:, :, :], c_tanh[:, :].rearrange("p (k b) -> p k b", k=KT), 0.5, None,
                              ALU.mult).then_inc(c_s, 1)
            mod_ps = b_qk[:, 0:2 * KT * B].rearrange("p (m b) -> p m b", b=B)

            def prep(b, piece):
                if piece == "normalise":
                    dve.wait_ge(ln_rstd, b + 1 if isinstance(b, int) else 3)
                    if not isinstance(b, int) or b > 0:
                        dve.wait_ge(ln_lo, b)
                    for t in range(TT):
                        tile = bass.ds(b * TT + t, 1)
                        dve.tensor_scalar(hmod[:, t, :], xs[:, tile, :].squeeze(1),
                                          mv[:, tile, 0:1].squeeze(1), rstd[:, tile],
                                          ALU.subtract, ALU.mult).then_inc(ln_z, 1)
                    if isinstance(b, int) and b == 0:
                        chunks([0])
                        dve.wait_ge(mod_mm, 1)
                        dve.tensor_copy(modT[:, 0:KT, :], mod_ps[:, 0:KT, :]).then_inc(mod_done, 1)
                        dve.tensor_scalar(modT[:, KT:2 * KT, :], mod_ps[:, KT:2 * KT, :], 1.0, None, ALU.add) \
                            .then_inc(mod_done, 1)
                        dve.wait_ge(mod_done, 2)
                        dve.wait_ge(rope_in, 16)
                if piece == "modulate":
                    dve.wait_ge(ln_hi, b * KT + KT)
                    for kt in range(KT):
                        dve.tensor_scalar(hmod[:, kt, :], b_ln[:, kt * S:(kt + 1) * S],
                                          modT[:, KT + kt, bass.ds(b, 1)], modT[:, kt, bass.ds(b, 1)],
                                          ALU.mult, ALU.add).then_inc(ln_mod, 1)

            def chunks(places):
                for n in places:
                    dve.wait_ge(w_hi, n + 1)
                    low_half(weights_chunk(1, ORDER[n]), stage[:, 1 + n % STAGES, :], W_UP,
                             weights_chunk(0, ORDER[n])) \
                        .then_inc(w_lo, 1)
            assert O_UP == G_UP
            unit = 1.0 / (W_UP * O_UP)

            def first(i):
                chunks(chunks_before(i))
                if i == -2:
                    dve.wait_ge(g_mm, 1)
                    dve.tensor_scalar(m_row[:, 2, :], b_pv[0:B, 0:D], 1.0, None, ALU.add).then_inc(g_done, 1)
                    dve.tensor_copy(m_row[:, 3, :], b_pv[0:B, D:2 * D]).then_inc(g_done, 1)
                if i == -1:
                    dve.tensor_scalar(g_sign[:, :], b_ln[0:B, :], 0.0, 2.0 * unit, ALU.is_ge, ALU.mult) \
                        .then_inc(mod_sb, 1)
                    dve.tensor_scalar(g_abs[:, :], b_ln[0:B, :], -1.0, GATE_FLOOR, ALU.mult, ALU.max) \
                        .then_inc(mod_sb, 1)
                if i == 0:
                    dve.wait_ge(mod_sb, 2)
                    dve.tensor_tensor(g_abs[:, :], b_ln[0:B, :], g_abs[:, :], ALU.max).then_inc(mod_sb, 1)
                    dve.wait_ge(mod_sb, 3)
                    dve.scalar_tensor_tensor(out=m_row[:, 0:2, :],
                                             in0=g_sign[:, :].rearrange("b (k n) -> b k n", k=2),
                                             scalar=-unit, in1=g_abs[:, :].rearrange("b (k n) -> b k n", k=2),
                                             op0=ALU.add, op1=ALU.mult).then_inc(g_done, 1)
                if i == -1:
                    dve.wait_ge(scattered, 16)
                    dve.tensor_copy(base[:, :], t_base)
                    dve.wait_ge(x_rest_in, 16)
                    statistics(TT, 2 * TT)
                b = i - (H - 1) + B
                if 2 <= b < B:
                    statistics(b * TT, (b + 1) * TT)

            qk4 = b_qk[:, :].rearrange("p (a f d) -> p a f d", a=TT * 2, f=2)

            def part_low(part):
                dve.wait_ge(fw_hi, part + 1)
                low_half(split16[:, 1, :], stage[:, 0, 0:FPART], W_UP, split16[:, 0, :]).then_inc(fw_lo, 1)

            def step(i, j, b, h, g):
                if exists(i, 1):
                    k = (j + 1) % 2
                    dve.wait_ge(exped, i + 2)
                    wait(dve, normed, i)
                    dve.reciprocal(rsum[:, k, :], esum[:, k, :]).then_inc(rsummed, 1)
                if exists(i, 2):
                    dve.wait_ge(t_hi, i + 3)
                    low_half(qkT[:, j % 2, 1, :], b_t[:, :], 1.0, qkT[:, j % 2, 0, :]).then_inc(t_lo, 1)
                if exists(i, 3):
                    k = (j + 3) % 4
                    dve.wait_ge(v_hi, i + 4)
                    low_half(v16[:, k, 1, :], b_v[:, 0:TT * DH], V_UP / W_UP, v16[:, k, 0, :]) \
                        .then_inc(v_lo, 1)
                if exists(i, 4):
                    k = j % 2
                    dve.wait_ge(qk_copied, i + 5)
                    wait(dve, t_mm, i + 3)
                    r4 = rot[:, k, :].rearrange("p (a f d) -> p a f d", a=TT * 2, f=2)
                    s4 = rope_sb[:, 1, :].rearrange("p (a f d) -> p a f d", a=TT * 2, f=2)
                    dve.tensor_tensor(r4[:, :, 0, :], qk4[:, :, 1, :], s4[:, :, 0, :], ALU.mult)
                    dve.tensor_tensor(r4[:, :, 1, :], qk4[:, :, 0, :], s4[:, :, 1, :], ALU.mult) \
                        .then_inc(rot_done, 1)
                if exists(i, 0):
                    dve.wait_ge(o_hi, i + 1)
                    low_half(head_out(1, h), b_pv[:, 0:S], O_UP / (P_UP * V_UP), head_out(0, h)) \
                        .then_inc(o_lo, 1)
                if exists(i, 2):
                    dve.wait_ge(s_mm, i + 3)
                    wait(dve, exped, i + 1)
                    dve.tensor_reduce(nmax[:, j % 2, :], b_s[:, :].rearrange("p (t s) -> p t s", t=TT),
                                      AX.X, ALU.max, negate=True).then_inc(maxed, 1)
                if exists(i, 1):
                    dve.wait_ge(pt_hi, i + 2)
                    low_half(pT[:, 1, :, :], b_pt[:, :].rearrange("p (k s) -> p k s", k=KT), P_UP,
                             pT[:, 0, :, :]).then_inc(pt_lo, 1)
                if j == HQ - 1 and exists(i, 0):
                    part_low(b * NG + g)

            def table(stage, early):
                steps = [TABLE_AT[stage][0] if early else TABLE_OPS + TABLE_AT[stage][1]]

                def link(ins):
                    steps[0] += 1
                    ins.then_inc(bt, 1)
                    dve.wait_ge(bt, steps[0])

                first = 0 if early else EARLY
                n = EARLY if early else NB - EARLY
                blocks = slice(first, first + n)

                def over_blocks(v):
                    return v.unsqueeze(1).to_broadcast([P, n, E])

                if stage == "count":
                    link(dve.tensor_tensor(cnt[:, :], base[:, :], t_base, ALU.subtract))
                    ks = slice(1, NT) if early else slice(0, NT)
                    link(dve.tensor_tensor(over[:, :, ks],
                                           cnt[:, :].unsqueeze(2).to_broadcast([P, E, ks.stop - ks.start]),
                                           t_thr[:, :, ks], ALU.is_ge if early else ALU.is_gt))
                    link(dve.tensor_reduce(cnt[:, :], over[:, :, ks], AX.X, ALU.add))
                    if not early:
                        link(dve.tensor_tensor(cnt[:, :], cnt[:, :], gone[:, :], ALU.subtract))
                    link(dve.tensor_copy(ends[:, 0, :], cnt[:, :]))
                if stage == "sum":
                    q = 0
                    for d in (1, 2, 4):
                        link(dve.tensor_copy(ends[:, 1 - q, 0:d], ends[:, q, 0:d]))
                        link(dve.tensor_tensor(ends[:, 1 - q, d:E], ends[:, q, d:E], ends[:, q, 0:E - d], ALU.add))
                        q = 1 - q
                    assert q == 1
                if stage == "shifts":
                    link(dve.tensor_tensor(shift[:, :], ends[:, 1, :], cnt[:, :], ALU.subtract))
                    if early:
                        link(dve.tensor_scalar(gone[:, :], shift[:, :], -1.0, float(EARLY), ALU.mult, ALU.add))
                        link(dve.scalar_tensor_tensor(out=gone[:, :], in0=gone[:, :], scalar=0.0, in1=cnt[:, :],
                                                      op0=ALU.max, op1=ALU.min))
                    else:
                        link(dve.tensor_tensor(shift[:, :], shift[:, :], gone[:, :], ALU.subtract))
                    link(dve.scalar_tensor_tensor(out=shift[:, :], in0=shift[:, :], scalar=float(P), in1=t_base,
                                                  op0=ALU.mult, op1=ALU.subtract))
                if stage == "experts":
                    link(dve.tensor_tensor(bcmp[:, 0:n, :], t_blk[:, 0:n, :], over_blocks(ends[:, 1, :]),
                                           ALU.is_ge))
                    link(dve.tensor_reduce(bexp[:, 0:n], bcmp[:, 0:n, :], AX.X, ALU.add))
                    link(dve.tensor_scalar(bexp[:, 0:n], bexp[:, 0:n], E - 1.0, None, ALU.min))
                if stage == "first rows":
                    link(dve.tensor_tensor(bcmp[:, 0:n, :], t_exp[:, 0:n, :],
                                           bexp[:, 0:n].unsqueeze(2).to_broadcast([P, n, E]), ALU.is_equal))
                    link(dve.tensor_tensor(bcmp[:, 0:n, :], bcmp[:, 0:n, :], over_blocks(shift[:, :]), ALU.mult))
                    link(dve.tensor_reduce(brow[:, 0:n], bcmp[:, 0:n, :], AX.X, ALU.add))
                    link(dve.scalar_tensor_tensor(out=brow[:, 0:n], in0=t_blk[:, 0:n, 0], scalar=float(P),
                                                  in1=brow[:, 0:n], op0=ALU.mult, op1=ALU.subtract))
                    link(dve.tensor_scalar(btab[:, 1, blocks], brow[:, 0:n], base[:, E - 1:E], None, ALU.min))
                    link(dve.tensor_scalar(bfirst[:, blocks], bexp[:, 0:n], -1.0, float(E), ALU.mult, ALU.add))
                    dve.tensor_copy(btab[:, 0, blocks], bexp[:, 0:n]).then_inc(btab_done, 1)
                    assert steps[0] == (TABLE_OPS if early else 2 * TABLE_OPS)

            def late(b, piece):
                tiles = bass.ds(b * TT, TT)
                done = [CHAIN.get(piece, 0)]

                def link(ins):
                    done[0] += 1
                    ins.then_inc(rt, 1)
                    dve.wait_ge(rt, b * ROUTE_OPS + done[0])

                if isinstance(b, int) and b == B - 2 and LATE.index(piece) in EARLY_TABLE:
                    table(EARLY_TABLE[LATE.index(piece)], early=True)
                if piece in TABLE_AT:
                    table(piece, early=False)
                if piece == "gate":
                    dve.wait_ge(o_mm, b + 1)
                    dve.wait_ge(m_in, (b + 1) * 16)
                    dve.tensor_tensor(gated[:, :, :], b_acc[:, :].rearrange("p (t n) -> p t n", t=TT),
                                      mB[:, 0:1, :].to_broadcast([P, TT, D]), ALU.mult) \
                        .then_inc(gate_done, 1)
                if piece == "add":
                    dve.wait_ge(gate_done, b + 1)
                    dve.tensor_tensor(z[:, :, :], xs[:, tiles, :], gated[:, :, :], ALU.add) \
                        .then_inc(x1_done, 1)
                if piece == "statistics":
                    dve.wait_ge(x1_done, b + 1)
                    for t in range(TT):
                        dve.bn_stats(stats[:, t, :], z[:, t, :]).then_inc(l2_stat, 1)
                if piece == "moments":
                    dve.wait_ge(l2_stat, (b + 1) * TT)
                    dve.tensor_tensor(xs[:, tiles, :], xs[:, tiles, :], gated[:, :, :], ALU.add)
                    for t in range(TT):
                        dve.bn_aggr(mv[:, t, :], stats[:, t, :]).then_inc(l2_mv, 1)
                    dve.wait_ge(l2_mv, b * (TT + 1) + TT)
                    dve.tensor_scalar(mv[:, 0:TT, 1], mv[:, 0:TT, 1], EPS, None, ALU.add).then_inc(l2_mv, 1)
                if piece == "normalise":
                    dve.wait_ge(l2_rstd, b + 1)
                    for t in range(TT):
                        dve.tensor_scalar(z[:, t, :], z[:, t, :], mv[:, t, 0:1], rstd[:, t:t + 1],
                                          ALU.subtract, ALU.mult).then_inc(l2_z, 1)
                if piece == "first":
                    dve.wait_ge(logit_mm, b + 1)
                    dve.tensor_scalar(h2[:, :, D], t_token[:, tiles], 1.0, None, ALU.mult)
                    link(dve.tensor_copy(lg[:, 0, :, :], b_ln[:, 0:TT * E].rearrange("p (t e) -> p t e", e=E)))
                if piece in ("first", "second"):
                    q = ("first", "second").index(piece)
                    best = (h2[:, :, D + 1], second[:, :])[q]
                    link(dve.tensor_reduce(top[:, q, :], lg[:, q, :, :], AX.X, ALU.max))
                    link(dve.tensor_tensor(hit[:, :, :], lg[:, q, :, :],
                                           top[:, q, :].unsqueeze(2).to_broadcast([P, TT, E]), ALU.is_equal))
                    link(dve.tensor_tensor(hit[:, :, :], hit[:, :, :], t_first, ALU.mult))
                    link(dve.tensor_reduce(best, hit[:, :, :], AX.X, ALU.max))
                    link(dve.tensor_tensor(sel[:, q, :, :], hit[:, :, :],
                                           best.unsqueeze(2).to_broadcast([P, TT, E]), ALU.is_equal))
                if piece == "first":
                    link(dve.scalar_tensor_tensor(out=lg[:, 1, :, :], in0=sel[:, 0, :, :], scalar=-FAR,
                                                  in1=lg[:, 0, :, :], op0=ALU.mult, op1=ALU.add))
                topb = top[:, :, :].unsqueeze(3).to_broadcast([P, 2, TT, E])
                if piece == "both":
                    link(dve.tensor_tensor(m16[:, :, :], sel[:, 0, :, :], sel[:, 1, :, :], ALU.add))
                    assert done[0] == M16_AT
                    link(dve.tensor_tensor(diff[:, :, :, :], lg[:, :, :, :], topb, ALU.subtract))
                    assert done[0] == EXP_AT
                    link(dve.scalar_tensor_tensor(out=absl[:, :, :, :], in0=lg[:, :, :, :], scalar=-1.0,
                                                  in1=lg[:, :, :, :], op0=ALU.mult, op1=ALU.max))
                if piece == "kept":
                    link(dve.tensor_tensor(absl[:, :, :, :], absl[:, :, :, :], topb, ALU.max))
                    link(dve.scalar_tensor_tensor(out=keep[:, :, :, :], in0=absl[:, :, :, :], scalar=-JITTER,
                                                  in1=diff[:, :, :, :], op0=ALU.mult, op1=ALU.is_le))
                ranks = b_ln[:, 32:32 + (TT + 1) * E].rearrange("p (t e) -> p t e", e=E)
                if piece == "weights":
                    dve.wait_ge(rt_exp, b + 1)
                    link(dve.tensor_tensor(keep[:, :, :, :], keep[:, :, :, :], ediff[:, :, :, :], ALU.mult))
                    link(dve.tensor_reduce(psum_[:, :, :], keep[:, :, :, :], AX.X, ALU.add))
                    link(dve.reciprocal(wts[:, :, tiles], psum_[:, :, :]))
                    dve.wait_ge(rank_mm, b + 1)
                    link(dve.tensor_tensor(row[:, :, :], ranks[:, 0:TT, :],
                                           base[:, :].unsqueeze(1).to_broadcast([P, TT, E]), ALU.add))
                    link(dve.tensor_tensor(base[:, :], base[:, :], ranks[:, TT, :], ALU.add))
                    if isinstance(b, int) and b == B - 1:
                        dve.tensor_copy(free_i[:, :], base[:, :]).then_inc(tails, 1)
                if piece == "rows":
                    for q in range(2):
                        link(dve.tensor_tensor(srow[:, q, :, :], sel[:, q, :, :], row[:, :, :], ALU.mult))
                    link(dve.tensor_reduce(slot[:, :, :], srow[:, :, :, :], AX.X, ALU.add))
                    link(dve.tensor_scalar(slot_i[:, :, :], slot[:, :, :], 1.0, None, ALU.mult))
                    assert done[0] == ROUTE_OPS

            run_heads(step, late, prep, first, dve)

            def ffn(k, j, r, part):
                if has(k, 0):
                    dve.wait_ge(coded, k + 1)
                    wait(dve, y_st[j], r * 16)
                    dve.tensor_scalar(code_i[:, j:j + 1], code[:, bass.ds(k, 1)], 1.0, None, ALU.mult) \
                        .then_inc(code_out, 1)
                    dve.wait_ge(g_hi, k + 1)
                    low_half(gT[:, 1, :, :], b_pt[:, :].rearrange("p (k s) -> p k s", k=FT),
                             G_UP / (2 * W_UP * W_UP), gT[:, 0, :, :]).then_inc(g_lo, 1)
                if has(k, 2):
                    col = bass.ds(k + 2, 1)
                    dve.wait_ge(xg_in[j], r * 16 + 32)
                    dve.tensor_scalar(code[:, col], xg[:, j, D + 1:D + 2], bfirst[:, col], T + 1.0,
                                      ALU.not_equal, ALU.mult).then_inc(coding, 1)
                    dve.scalar_tensor_tensor(out=spare[:, j:j + 1], in0=xg[:, j, D:D + 1], scalar=0.0,
                                             in1=t_spare[:, col], op0=ALU.is_equal, op1=ALU.mult) \
                        .then_inc(coding, 1)
                    dve.wait_ge(coding, k * 2 + 6)
                    dve.scalar_tensor_tensor(out=code[:, col], in0=code[:, col], scalar=xg[:, j, D:D + 1],
                                             in1=spare[:, j:j + 1], op0=ALU.add, op1=ALU.add) \
                        .then_inc(coded, 1)
                    dve.wait_ge(x_hi, k + 3)
                    low_half(xT[:, j, 1, :, :], b_t[:, 0:D].rearrange("p (k s) -> p k s", k=KT), 1.0,
                             xT[:, j, 0, :, :]).then_inc(x_lo, 1)
                if has(k, 1):
                    dve.wait_ge(tanhed, k + 2)
                    wait(dve, gg_done, k + 1)
                    dve.scalar_tensor_tensor(out=ua[:, :], in0=th[:, :], scalar=1.0, in1=b_a[(j + 1) % 2][:, :],
                                             op0=ALU.add, op1=ALU.mult).then_inc(u_done, 1)
                if has(k, 1):
                    dve.wait_ge(u_done, k + 2)
                    dve.wait_ge(b_mm, k + 2)
                    dve.tensor_tensor(gg[:, :], ua[:, :], b_s[:, :], ALU.mult).then_inc(gg_done, 1)

            all_blocks(ffn, late, dve)
            def add_result(b):
                rows = xs[:, b * TT:(b + 1) * TT, :]
                dve.wait_ge(fin_gated, b + 1)
                dve.tensor_tensor(rows, rows, yg[:, b, 1, :, :], ALU.add).then_inc(fin_done, 1)

            for b in range(B):
                for t in range(TT):
                    y = yg[:, b, :, t, :]
                    tile = b * TT + t
                    dve.wait_ge(fin_first, tile + 1)
                    dve.scalar_tensor_tensor(out=y[:, 1, :], in0=y[:, 1, :], scalar=wts[:, 1, tile:tile + 1],
                                             in1=y[:, 0, :], op0=ALU.mult, op1=ALU.add).then_inc(fin_both, 1)
                if b > 0:
                    add_result(b - 1)
            add_result(B - 1)

        @block.tensor
        def _(pe):
            pe.wait_ge(c_s, 2)
            pe.wait_ge(wmod_in, 16)
            for j in range(2 * KT):
                for kt in range(KT):
                    m = pe.matmul(b_qk[:, j * B:(j + 1) * B], wmod_sb[:, kt, j * P:(j + 1) * P],
                                  c_silu[:, kt, :], start=(kt == 0), stop=(kt == KT - 1))
            m.then_inc(mod_mm, 1)
            pe.wait_ge(consts, 7)

            def first(i):
                if i == -3:
                    pe.wait_ge(wmod_rest_in, 16)
                    for ps, kinds in ((b_ln, (2, 5)), (b_pv, (4, 3))):
                        for g, kind in enumerate(kinds):
                            for kt in range(KT):
                                m = pe.matmul(ps[0:B, g * D:(g + 1) * D], c_silu[:, kt, :],
                                              wmod_sb[:, kt, kind * D:(kind + 1) * D], start=(kt == 0),
                                              stop=(kt == KT - 1))
                    m.then_inc(g_mm, 1)
                if i == 0:
                    pe.wait_ge(small_in, 16)
                if i == -HQ or chunks_for(i) > chunks_for(i - 1):
                    pe.wait_ge(w_lo, chunks_for(i))

            def prep(b, piece):
                if piece == "transpose":
                    pe.wait_ge(ln_z, b * TT + TT)
                    for kt in range(KT):
                        for t in range(TT):
                            m = pe.transpose(b_ln[:, kt * S + t * P:kt * S + (t + 1) * P],
                                             hmod[:, t, kt * P:(kt + 1) * P], ident[:, :])
                    m.then_inc(ln_t, 1)

            def product(out, stat, mov, n=KT):
                for q, (a, c_) in enumerate(PASSES):
                    for k in range(n):
                        m = pe.matmul(out, stat(a, k), mov(c_, k), start=(q == 0 and k == 0),
                                      stop=(q == len(PASSES) - 1 and k == n - 1))
                return m

            def tokens(b, t):
                return lambda a, k: hT[:, a, b, k, t * P:(t + 1) * P] if isinstance(b, int) else \
                    hT[:, a, bass.ds(b, 1), k, t * P:(t + 1) * P].squeeze(1)

            def weights(h, first, step, width):
                start = h * (3 * KT * DH) + first
                return lambda a, k: qkv16[:, a, bass.ds(start + k * step, width)]

            def project(i, b, h):
                pe.wait_ge(o_lo, i + 1)
                if h == 0 and not (isinstance(b, int) and b == 0):
                    pe.wait_ge(gate_done, b)
                for t in range(TT):
                    for q, (a, c_) in enumerate(PASSES):
                        m = pe.matmul(b_acc[:, t * D:(t + 1) * D], oT[:, a, h, t * P:(t + 1) * P],
                                      wo16[:, c_, h, :], start=(h == 0 and q == 0 and t == 0),
                                      stop=(h == H - 1 and q == len(PASSES) - 1 and t == TT - 1))
                if h == H - 1:
                    m.then_inc(o_mm, 1)

            def step(i, j, b, h, g):
                if exists(i, 2):
                    pe.wait_ge(rope_done, i + 3)
                    wait(pe, t_lo, i + 2)
                    for a in range(2):
                        for t in range(TT):
                            m = pe.transpose(b_t[:, a * S + t * P:a * S + (t + 1) * P],
                                             rot[:, j % 2, (t * 2 + a) * DH:(t * 2 + a + 1) * DH], ident[:, :])
                    m.then_inc(t_mm, 1)
                if exists(i, 3):
                    bb, hh = at(i, b, h, 3)
                    wait(pe, v_lo, i + 3)
                    for t in range(TT):
                        m = product(b_v[:, t * DH:(t + 1) * DH], tokens(bb, t),
                                    weights(hh, 2 * KT * DH, DH, DH))
                    m.then_inc(v_mm, 1)
                if exists(i, 4):
                    bb, hh = at(i, b, h, 4)
                    if isinstance(hh, int) and hh == 0:
                        pe.wait_ge(ln_lo, bb + 1)
                    wait(pe, rot_done, i + 4)
                    for t in range(TT):
                        m = product(b_qk[:, t * 2 * DH:(t + 1) * 2 * DH], tokens(bb, t),
                                    weights(hh, 0, 2 * DH, 2 * DH))
                    m.then_inc(qk_mm, 1)

                if exists(i, -1):
                    if h > 0:
                        project(i - 1, b, h - 1)
                    else:
                        project(i - 1, b - 1, H - 1)
                if exists(i, 0):
                    pe.wait_ge(pt_lo, i + 1)
                    pe.wait_ge(v_lo, i + 1)
                    wait(pe, o_lo, i)
                    product(b_pv[:, 0:S], lambda a, k: v16[:, j % 4, a, k * DH:(k + 1) * DH],
                            lambda a, k: pT[:, a, k, :]).then_inc(pv_mm, 1)
                if exists(i, 2):
                    q2 = j % 2
                    pe.wait_ge(t_lo, i + 3)
                    wait(pe, exped, i + 2)
                    for t in range(TT):
                        m = product(b_s[:, t * S:(t + 1) * S],
                                    lambda a, k: qkT[:, q2, a, t * P:(t + 1) * P],
                                    lambda a, k: qkT[:, q2, a, S:2 * S], 1)
                    m.then_inc(s_mm, 1)
                if exists(i, 1):
                    pe.wait_ge(normed, i + 2)
                    wait(pe, pt_lo, i + 1)
                    for k in range(KT):
                        for t in range(TT):
                            m = pe.transpose(b_pt[:, k * S + t * P:k * S + (t + 1) * P],
                                             ex[:, (j + 1) % 2, t, k * P:(k + 1) * P], ident[:, :])
                    m.then_inc(pt_mm, 1)
            def late(b, piece):
                if piece == "project":
                    project(b * H + H - 1, b, H - 1)
                if piece == "transpose":
                    pe.wait_ge(h2_done, b * 2 + 2)
                    for kt in range(KT):
                        for t in range(TT):
                            m = pe.transpose(b_ln[:, kt * S + t * P:kt * S + (t + 1) * P],
                                             h2[:, t, kt * P:(kt + 1) * P], ident[:, :])
                    m.then_inc(h2_t, 1)
                if piece == "logits":
                    pe.wait_ge(h2_copy, b + 1)
                    for t in range(TT):
                        for kt in range(KT):
                            m = pe.matmul(b_ln[:, t * E:(t + 1) * E], h2T[:, kt, t * P:(t + 1) * P],
                                          gw_sb[:, kt * E:(kt + 1) * E], start=(kt == 0), stop=(kt == KT - 1))
                    m.then_inc(logit_mm, 1)
                if piece == "kept":
                    pe.wait_ge(rt, b * ROUTE_OPS + M16_AT)
                    for t in range(TT + 1):
                        for k in range(min(t + 1, TT)):
                            m = pe.matmul(b_ln[:, 32 + t * E:32 + (t + 1) * E],
                                          (tri16 if k == t else ones16)[:, :], m16[:, k, :],
                                          start=(k == 0), stop=(k == min(t, TT - 1)))
                    m.then_inc(rank_mm, 1)

            run_heads(step, late, prep, first, pe)
            pe.wait_ge(btab_done, 1)

            last = [None]

            def expert(k):
                return pe.value_load(btab[0:1, 0, bass.ds(k, 1)], min_val=0, max_val=E - 1)

            def ffn(k, j, r, part):
                if has(k, 2):
                    pe.wait_ge(xg_in[j], r * 16 + 32)
                    wait(pe, x_lo, k + 2)
                    for kt in range(KT):
                        m = pe.transpose(b_t[:, kt * P:(kt + 1) * P], xg[:, j, kt * P:(kt + 1) * P], ident[:, :])
                    m.then_inc(xt_mm, 1)
                if has(k, 0):
                    pe.wait_ge(gg_done, k + 1)
                    wait(pe, g_lo, k)
                    for q in range(FT):
                        m = pe.transpose(b_pt[:, q * P:(q + 1) * P], gg[:, q * P:(q + 1) * P], ident[:, :])
                    m.then_inc(gt_mm, 1)
                stat = lambda a, q: xT[:, (j + 1) % 2, a, q, :]
                if has(k, 1):
                    e1 = expert(k + 1)
                    col = e1 * (2 * FW)
                    pe.wait_ge(w_ffn, e1 * 32 + 32)
                    pe.wait_ge(x_lo, k + 2)
                    wait(pe, u_done, k)
                    product(b_a[(j + 1) % 2][:, :], stat,
                            lambda a, q: arena[:, bass.ds(col + (a * FW + q * F), F)]).then_inc(a_mm, 1)
                if has(k, 1):
                    product(b_s[:, :], stat,
                            lambda a, q: arena[:, bass.ds(col + (a * FW + KT * F + q * F), F)]) \
                        .then_inc(b_mm, 1)
                if has(k, 0):
                    col0 = (last[0] if part > 0 and last[0] is not None else expert(k)) * (2 * FW)
                    pe.wait_ge(g_lo, k + 1)
                    wait(pe, y_out, k)
                    product(b_pv[:, 0:D], lambda a, q: gT[:, a, q, :],
                            lambda a, q: arena[:, bass.ds(col0 + (a * FW + 2 * KT * F + q * D), D)], FT) \
                        .then_inc(y_mm, 1)
                last[0] = e1 if has(k, 1) else None

            all_blocks(ffn, late, pe)


def kernel(**inputs):
    import numpy as np
    import concourse.bacc as bacc
    from concourse.bass_utils import run_bass_kernel_spmd as run

    a = {k: np.asarray(v) for k, v in inputs.items()}
    x = a["L0_attn_x"].reshape(T, D)
    c = a["L0_c"].T.reshape(KT, P, B).transpose(1, 0, 2).reshape(P, KT * B)
    wmod = a["L0_wmod"].reshape(KT, P, NMOD * D).transpose(1, 0, 2)
    w = a["L0_attn_w_qkv"].reshape(3, H, DH, KT, P)
    qk = w[:2].transpose(4, 1, 3, 0, 2).reshape(P, H, KT * 2 * DH)
    v = w[2].transpose(3, 0, 2, 1).reshape(P, H, KT * DH)
    wo = a["L0_attn_w_out"].reshape(D, H, DH).transpose(2, 1, 0).reshape(P, H * D)
    wall = np.concatenate([np.concatenate([qk, v], axis=2).reshape(P, WCOLS), wo], axis=1)
    half = np.arange(0, DH, 2, dtype=np.float32) / np.float32(DH)
    inv = (1.0 / np.float32(10000.0) ** half).astype(np.float32)
    ang = np.arange(S, dtype=np.float32)[:, None] * inv[None, :]
    up = float(DH) ** -0.25 / W_UP
    cos, sin = np.cos(ang) * up, np.sin(ang) * up
    cos2 = np.concatenate([cos, cos], 1).reshape(TT, P, DH)
    sin2 = np.concatenate([-sin, sin], 1).reshape(TT, P, DH)
    rope = np.stack([np.repeat(t.transpose(1, 0, 2)[:, :, None], 2, axis=2).reshape(P, TT * 2 * DH)
                     for t in (cos2, sin2)], 1).astype(np.float32)
    gate_w = a["L0_ffn_gate_w"].reshape(E, KT, P).transpose(2, 1, 0).reshape(P, KT * E)
    w1, w3 = (a[k].reshape(E, F, KT, P).transpose(0, 3, 2, 1).reshape(E, P, KT * F)
              for k in ("L0_ffn_w1", "L0_ffn_w3"))
    w2 = a["L0_ffn_w2"].reshape(E, D, FT, P).transpose(0, 3, 2, 1).reshape(E, P, FT * D)
    fw = np.concatenate([w1, w3, w2], axis=2)
    e, blk = np.arange(E), np.arange(NB)
    table = np.concatenate([np.tile(E - e, TT), e * XS, np.tile(P * np.arange(NT), E),
                            np.repeat(blk, E), np.tile(e, NB)]).astype(np.float32)
    token = np.arange(T, dtype=np.float32).reshape(NT, P).T + 1
    spare = np.arange(NB * P, dtype=np.float32).reshape(NB, P).T + YR - (T + 1)
    table = np.concatenate([np.tile(table, (P, 1)), token, spare], axis=1)
    assert table.shape == (P, TABLE)
    data = {"in_x": x, "in_c": c, "in_wmod": wmod, "in_rope": rope, "in_wall": wall,
            "in_gate_w": gate_w, "in_fw": fw, "in_table": table}
    data = {k: np.ascontiguousarray(t) for k, t in data.items()}
    nc = bacc.Bacc("TRN2", target_bir_lowering=False, num_devices=1)
    aps = [nc.dram_tensor(k, t.shape, F32, kind="ExternalInput").ap() for k, t in data.items()]
    out = nc.dram_tensor("out_x", (B, S, D), F32, kind="ExternalOutput").ap()
    scratch = [nc.dram_tensor(k, shape, dt, kind="Internal").ap() for k, shape, dt in (
        ("mod_rows", (B, 4 * D), F32), ("ffn_halves", (E, P, 2, FW), F16),
        ("expert_rows", (E * XS, XW), F32), ("result_rows", (YR + NB * P, D), F32))]
    build(nc, *aps, out, *scratch)
    r = run(nc, [data], core_ids=[0])
    return r.results[0]["out_x"]
```
